# Optimizing a Trainium2 kernel written in Bass

```python
import numpy as np
import jax
import jax.numpy as jnp

def _softmax(x, axis=-1):
    return jax.nn.softmax(x, axis=axis)

def _gelu(x):
    return jax.nn.gelu(x, approximate=True)

def _silu(x):
    return jax.nn.silu(x)

def _sigmoid(x):
    return jax.nn.sigmoid(x)

def _layernorm(x, axis=-1, eps=1e-05):
    m = jnp.mean(x, axis=axis, keepdims=True)
    v = jnp.var(x, axis=axis, keepdims=True)
    return (x - m) / jnp.sqrt(v + eps)

def _scatter_add(tgt, idx, src, axis=0):
    return tgt.at[idx].add(src)

def _segment_sum(src, seg, n):
    return jax.ops.segment_sum(src, seg, n)
kernel_name = 'mk_gnn_preln_d2_gnn_r8_c01074'

def setup_inputs(seed: int=0):
    np.random.seed(seed)
    _w = jnp.asarray

    def _rec_inputs():
        import jax
        import jax.numpy as jnp
        _gk = jax.random.key(seed)
        x = -0.0005121 + 1.001 * jax.random.normal(jax.random.fold_in(_gk, 1), (12500, 64), jnp.float32)
        _s = jax.random.randint(jax.random.fold_in(_gk, 2), (100000,), 0, 12500, jnp.int32)
        _d = jax.random.randint(jax.random.fold_in(_gk, 3), (100000,), 0, 12500, jnp.int32)
        _loop = jnp.arange(12500, dtype=jnp.int32)
        src = jnp.concatenate([_s, _d, _loop])
        dst = jnp.concatenate([_d, _s, _loop])
        _o = jnp.argsort(dst, stable=True)
        src = src[_o]
        dst = dst[_o]
        edge_attr_8 = 0.000398945 + 1.00003 * jax.random.normal(jax.random.fold_in(_gk, 12), (212500, 8), jnp.float32)
        edge_type_16 = jax.random.randint(jax.random.fold_in(_gk, 14), (212500,), 0, 16, jnp.int32)
        return (x, src, dst, edge_attr_8, edge_type_16)
    x, src, dst, edge_attr_8, edge_type_16 = _rec_inputs()

    def _L0_gnn_setup():
        import jax, jax.numpy as jnp
        import numpy as np
        N_NODES = 6250
        N_EDGES = 100000
        D_IN = 64
        D_OUT = 64
        NUM_RELS = 16
        key = jax.random.key(seed)
        k1, k2, k3, k4, k5 = jax.random.split(key, 5)
        feat = jax.random.normal(k1, (N_NODES, D_IN), dtype=jnp.float32)
        weight = jax.random.normal(k2, (NUM_RELS, D_IN, D_OUT), dtype=jnp.float32) * 0.05
        src = jax.random.randint(k3, (N_EDGES,), 0, N_NODES, dtype=jnp.int32)
        dst = jax.random.randint(k4, (N_EDGES,), 0, N_NODES, dtype=jnp.int32)
        etypes = jax.random.randint(k5, (N_EDGES,), 0, NUM_RELS, dtype=jnp.int32)
        return {'feat': feat, 'weight': weight, 'src': src, 'dst': dst, 'etypes': etypes}
    _L0_gnn_all = _L0_gnn_setup()
    _L0_gnn_in = {k: v for k, v in _L0_gnn_all.items() if k in ('weight',)}
    del _L0_gnn_all

    def _L1_gnn_setup():
        import jax, jax.numpy as jnp
        import numpy as np
        N_NODES = 6250
        E_EDGES = 100000
        IN_F = 64
        OUT_F = 64
        EDGE_F = 8
        key = jax.random.key(seed)
        ks = jax.random.split(key, 6)
        x = jax.random.normal(ks[0], (N_NODES, IN_F), dtype=jnp.float32)
        edge_index = jax.random.randint(ks[1], (2, E_EDGES), 0, N_NODES, dtype=jnp.int64)
        edge_attr = jax.random.normal(ks[2], (E_EDGES, EDGE_F), dtype=jnp.float32)
        fan_in1 = 2 * IN_F + EDGE_F
        W1 = jax.random.normal(ks[3], (fan_in1, OUT_F), dtype=jnp.float32) / np.sqrt(fan_in1)
        b1 = jnp.zeros((OUT_F,), dtype=jnp.float32)
        W2 = jax.random.normal(ks[4], (OUT_F, OUT_F), dtype=jnp.float32) / np.sqrt(OUT_F)
        b2 = jnp.zeros((OUT_F,), dtype=jnp.float32)
        return {'x': x, 'edge_index': edge_index, 'edge_attr': edge_attr, 'W1': W1, 'b1': b1, 'W2': W2, 'b2': b2}
    _L1_gnn_all = _L1_gnn_setup()
    _L1_gnn_in = {k: v for k, v in _L1_gnn_all.items() if k in ('W1', 'b1', 'W2', 'b2')}
    del _L1_gnn_all
    return {'x': x, 'src': src, 'dst': dst, 'edge_attr_8': edge_attr_8, 'edge_type_16': edge_type_16, 'L0_gnn_weight': _L0_gnn_in['weight'], 'L1_gnn_W1': _L1_gnn_in['W1'], 'L1_gnn_b1': _L1_gnn_in['b1'], 'L1_gnn_W2': _L1_gnn_in['W2'], 'L1_gnn_b2': _L1_gnn_in['b2']}

def reference(x, src, dst, edge_attr_8, edge_type_16, L0_gnn_weight, L1_gnn_W1, L1_gnn_b1, L1_gnn_W2, L1_gnn_b2):
    import jax
    import jax.numpy as jnp

    def _L0_gnn_ref(feat, weight, src, dst, etypes):
        import jax, jax.numpy as jnp
        import numpy as np
        N_NODES = 6250
        N_EDGES = 100000
        D_IN = 64
        D_OUT = 64
        NUM_RELS = 16
        num_rels = weight.shape[0]
        h_src = feat[src]
        msg = jnp.zeros((h_src.shape[0], weight.shape[2]), dtype=feat.dtype)
        for r in range(num_rels):
            mask = etypes == r
            msg = msg + h_src * mask[:, None].astype(feat.dtype) @ weight[r]
        out = jax.ops.segment_sum(msg, dst, num_segments=feat.shape[0])
        return out

    def _L1_gnn_ref(x, edge_index, edge_attr, W1, b1, W2, b2):
        import jax, jax.numpy as jnp
        import numpy as np
        N_NODES = 6250
        E_EDGES = 100000
        IN_F = 64
        OUT_F = 64
        EDGE_F = 8
        src, dst = (edge_index[0], edge_index[1])
        msg_input = jnp.concatenate([x[src], x[dst], edge_attr], axis=1)
        h = jax.nn.relu(msg_input @ W1 + b1)
        msg = h @ W2 + b2
        out = jax.ops.segment_sum(msg, dst, num_segments=x.shape[0])
        return out
    edge_index = jnp.stack([src, dst])
    h = jnp.maximum(_layernorm(x, axis=-1), 0.0)
    x = x + _L0_gnn_ref(h, L0_gnn_weight, src, dst, edge_type_16)
    h = jnp.maximum(_layernorm(x, axis=-1), 0.0)
    x = x + _L1_gnn_ref(h, edge_index, edge_attr_8, L1_gnn_W1, L1_gnn_b1, L1_gnn_W2, L1_gnn_b2)
    return x

_drawn_inputs = setup_inputs


def setup_inputs(seed=0):
    import zlib

    import numpy as np

    out = dict(_drawn_inputs(seed))
    spreads = {'L1_gnn_b1': (0.0, 0.1), 'L1_gnn_b2': (0.0, 0.1)}
    factors = {}
    for name, (base, spread) in spreads.items():
        noise = np.random.default_rng([zlib.crc32(name.encode()), seed]).standard_normal(out[name].shape)
        drawn = base * np.exp(spread * noise) if base else spread * noise
        out[name] = jnp.asarray(drawn.astype(out[name].dtype))
    for name, factor in factors.items():
        out[name] = (out[name] * factor).astype(out[name].dtype)
    return out
```

```python
import concourse.bass as bass
import concourse.mybir as mybir
from concourse.alu_op_type import AluOpType as ALU
from contextlib import ExitStack


def gnn_kernel(nc, x, src, dst, edge_attr, edge_type, rel_weight, w1, b1, w2, b2, out):
    fp32, bf16, i32 = mybir.dt.float32, mybir.dt.bfloat16, mybir.dt.int32
    ACT = mybir.ActivationFunctionType
    X = mybir.AxisListType.X
    ENG = mybir.EngineType

    P = 128
    N, D = x.shape
    E, F = edge_attr.shape
    R = rel_weight.shape[0]
    PAR = 2
    RP = R // PAR
    T = 8
    GE = T * P
    G = -(-E // GE)
    LAST = E - GE
    DUP = GE * (G - 1) - LAST
    HG = G // 2
    U = 4
    NIT = G // U
    W0 = 16
    W1N = P
    C0 = RP * W0
    NP, NI = 125, N // 125
    CI = 20
    NC = NI // CI
    SUB = 4
    KA = D + 1
    ACCN = N + P
    NT = E // P
    AHEAD = 4
    FAR = float(1 << 20)
    assert G % U == 0 and G % 2 == 0 and NI * NP == N and 0 < DUP and NI % CI == 0

    ctx = ExitStack()
    with ctx:
        def sb(name, shape, dt):
            return ctx.enter_context(nc.sbuf_tensor(name, shape, dt))

        def sem(name):
            return ctx.enter_context(nc.semaphore(name))

        def dram(name, shape, dt):
            return nc.dram_tensor(name, shape, dt, kind="Internal").ap()

        h_table = dram("h_table", (N, D), fp32)
        p_table = dram("p_table", (N, D), fp32)
        q_table = dram("q_table", (N + P, 3 * D), bf16)
        SROWS = P * (-(-(N + P) // P))
        sums0 = dram("sums0", (SROWS, KA), fp32)
        sums1 = dram("sums1", (SROWS, KA), fp32)

        acc = sb("acc", [P, ACCN], fp32)
        xs = sb("xs", [P, NI, D], fp32)
        src_tab = sb("src_tab", [P, G, T], i32)
        key0 = sb("key0", [P, G + 1, T], fp32)
        key1 = sb("key1", [P, G + 1, T], fp32)
        base_row = sb("base_row", [1, G, T], i32)
        start_row = sb("start_row", [1, G + 1], i32)
        idx = sb("idx", [P, U, T], i32)
        rows = sb("rows", [P, U, T, D], fp32)
        onehot = sb("onehot", [P, 2, T, PAR * C0], fp32)
        slots = sb("slots", [P, 2, T, C0], fp32)
        relus = sb("relus", [P, 2, T, KA], fp32)
        onehot_t = sb("onehot_t", [P, 2, T * P], bf16)
        attr = sb("attr", [P, U, T * F], fp32)
        attr_t = sb("attr_t", [T * F + 1, 2, P], fp32)
        q_win = sb("q_win", [P, U, 3 * D], bf16)
        pq = sb("pq", [P, CI, 2 * D], fp32)
        q_rest = sb("q_rest", [P, CI, D], fp32)
        q3 = sb("q3", [P, CI, 3, D], bf16)
        xc = sb("xc", [P, CI, D], fp32)
        sq = sb("sq", [P, CI, D], fp32)
        h = sb("h", [P, 2, CI, D], fp32)
        stat = sb("stat", [P, 4, CI], fp32)
        ident = sb("ident", [P, P], fp32)
        iota_i = sb("iota_i", [P, PAR * C0], i32)
        iota_f = sb("iota_f", [P, PAR * C0], fp32)
        ones = sb("ones", [P, 1], fp32)
        eps = sb("eps", [P, 1], fp32)
        zrows = sb("zrows", [P, 3 * D], bf16)
        w_pairs = sb("w_pairs", [P, RP, D], fp32)
        w_all = sb("w_all", [D, R, D], fp32)
        w_attr = sb("w_attr", [T * F + 1, T, D], fp32)
        w1ab = sb("w1ab", [P, 2, 2 * D], fp32)
        w2b = sb("w2b", [KA, D], fp32)
        extremes = sb("extremes", [P, 5], fp32)
        flag = sb("flag", [1, 1], i32)

        def edge_list(n, dt):
            v = acc[0:HG, n * 2 * GE:(n + 1) * 2 * GE]
            return (v.bitcast(i32) if dt == i32 else v).rearrange("g (a e) -> g a e", a=2)
        dst_i, src_i, typ_i = edge_list(0, i32), edge_list(1, i32), edge_list(2, i32)
        dst_f, par_i, typ_f = edge_list(3, fp32), edge_list(4, i32), edge_list(5, fp32)
        src_f, off0, key0_g, key1_g = edge_list(1, fp32), edge_list(4, fp32), edge_list(0, fp32), edge_list(2, fp32)

        acc_nodes = acc[:, 0:N].rearrange("k (p i) -> k i p", i=NI)
        flat_oh = onehot[:].rearrange("p a b c -> p (a b c)")
        stage_a = flat_oh[:, 0:CI * NP].rearrange("k (i p) -> k i p", p=NP)
        stage_b = pq[:].rearrange("p a b -> p (a b)")[:, 0:CI * NP].rearrange("k (i p) -> k i p", p=NP)
        h_t = flat_oh[:, CI * NP:CI * NP + CI // 2 * NP].rearrange("k (i p) -> k i p", p=NP)
        presum = slots[:].rearrange("p b t c -> p b (t c)")

        s_row = slots[:].rearrange("p b t c -> p (b t c)")
        s_prod = s_row[:, 0:R * D].rearrange("p (r m) -> p r m", m=D)
        s_eq, s_tri, s_tmp = flat_oh[:, 0:P], flat_oh[:, P:2 * P], flat_oh[:, 2 * P:3 * P]
        s_gt = flat_oh[:, 3 * P:4 * P]
        s_msg = flat_oh[:, 4 * P:4 * P + KA]
        s_comb = flat_oh[:, 5 * P:5 * P + KA]
        s_dstf, s_typf = flat_oh[:, 6 * P:6 * P + 1], flat_oh[:, 6 * P + 1:6 * P + 2]
        s_dup, s_row_f = flat_oh[:, 6 * P + 2:6 * P + 3], flat_oh[:, 6 * P + 3:6 * P + 4]
        s_spare, s_tail = flat_oh[:, 6 * P + 4:6 * P + 5], flat_oh[:, 6 * P + 5:6 * P + 6]
        s_mask = flat_oh[:, 6 * P + 8:6 * P + 8 + R]
        s_attr = flat_oh[:, 7 * P:7 * P + T * F]
        s_back = flat_oh[:, 9 * P:9 * P + KA]
        s_pre = flat_oh[:, 10 * P:10 * P + D]
        s_spare_i = idx[:, 0, 4:5]
        s_src, s_dst, s_typ, s_out_i = idx[:, 0, 0:1], idx[:, 0, 1:2], idx[:, 0, 2:3], idx[:, 0, 3:4]
        s_q = q_win[:, 0, :]

        ps = ctx.enter_context(nc.psum_tensor("ps", [P, 8, 512], fp32))
        ps_all = ps[:].rearrange("p a b -> p (a b)")
        slot_ps = ps_all[:, 0:4 * 512].rearrange("p (b t c) -> p b t c", b=2, t=T)
        node_ps = ps_all[0:D, 4 * 512:6 * 512].rearrange("k (b n) -> k b n", b=2)
        oht_ps = ps_all[:, 0:2 * 512]
        attrt_ps = ps[0:T * F, 2, 0:P]
        pre_ps = ps_all[:, 3 * 512:5 * 512].rearrange("p (b c) -> p b c", b=2)
        z_ps = ps_all[0:KA, 5 * 512:7 * 512].rearrange("k (b n) -> k b n", b=2)
        x_ps = ps_all[0:NP, 0:CI * D]
        ht_ps = ps_all[:, 3 * 512:3 * 512 + CI // 2 * P].rearrange("k (i p) -> k i p", p=P)
        pq_ps = ps[0:NP, 6:8, :]
        out_ps = [ps_all[0:NP, b * 3 * 512:b * 3 * 512 + CI * D] for b in range(2)]

        ids_in = [sem(f"ids_in_{k}") for k in range(3)]
        x_in = [sem(f"x_in_{k}") for k in range(NC)]
        weights_in = sem("weights_in")
        base_in = sem("base_in")
        consts_made = sem("consts_made")
        pool_chain = sem("pool_chain")
        dve_chain = sem("dve_chain")
        starts_made = sem("starts_made")
        src_float = sem("src_float")
        keys_made = sem("keys_made")
        keys_masked = sem("keys_masked")
        bad_made = sem("bad_made")
        bad_summed = sem("bad_summed")
        flag_made = sem("flag_made")
        prep_turned = sem("prep_turned")
        prep_copied = sem("prep_copied")
        centered = sem("centered")
        squared = sem("squared")
        var_made = sem("var_made")
        std_made = sem("std_made")
        h_made = sem("h_made")
        h_stored = [sem(f"h_stored_{b}") for b in range(2)]
        blocks_cleared = sem("blocks_cleared")
        idx0_in = [sem(f"idx0_in_{u}") for u in range(U)]
        rows0_in = [sem(f"rows0_in_{u}") for u in range(U)]
        onehot0 = sem("onehot0")
        slots_summed = sem("slots_summed")
        slots_copied = sem("slots_copied")
        typed = sem("typed")
        window_added = sem("window_added")
        layer0_summed = sem("layer0_summed")
        staged = sem("staged")
        turned = sem("turned")
        x_added = sem("x_added")
        h_turned = sem("h_turned")
        ht_copied = sem("ht_copied")
        pq_made = sem("pq_made")
        pq_copied = sem("pq_copied")
        q_split = sem("q_split")
        p_stored = sem("p_stored")
        q_stored = sem("q_stored")
        chunk_stored = sem("chunk_stored")
        idx1_in = [sem(f"idx1_in_{u}") for u in range(U)]
        q_in = [sem(f"q_in_{u}") for u in range(U)]
        attr_in = [sem(f"attr_in_{u}") for u in range(U)]
        rows1_in = [sem(f"rows1_in_{u}") for u in range(U)]
        onehot1 = sem("onehot1")
        group_turned = sem("group_turned")
        turn_copied = sem("turn_copied")
        pre_made = sem("pre_made")
        pre_added = sem("pre_added")
        relu_made = sem("relu_made")
        z_made = sem("z_made")
        z_added = sem("z_added")
        layer1_summed = sem("layer1_summed")
        out_staged = sem("out_staged")
        out_made = sem("out_made")
        out_added = sem("out_added")
        out_stored = sem("out_stored")
        sc = {(k, n): sem(f"scattered{n}_{k}") for n in range(2)
              for k in ("consts", "cleared", "zeroed", "ids", "gathered", "dst_float", "turned", "turn_copied", "made",
                        "masked", "summed", "placed", "added", "back_in", "back_turned", "back_copied", "chain")}

        waited = {e: sem(f"waited_{n}") for e, n in ((ENG.SP, "sync"), (ENG.Pool, "gpsimd"), (ENG.DVE, "vector"), (ENG.PE, "tensor"))}

        block = ctx.enter_context(nc.Block())

        class Chain:

            def __init__(self, eng, s, wait=None):
                self.eng, self.s, self.at, self.n = eng, s, 0, 0
                self.wait = wait or (lambda eng, s, value: eng.wait_ge(s, value))

            def __call__(self, ins):
                self.n += 1
                ins.then_inc(self.s, 1)
                self.wait(self.eng, self.s, self.at + self.n)

            def enter(self, i, k):
                self.before = self.at + self.n
                self.at, self.n, self.k = self.before + i * k, 0, k

            def leave(self, turns):
                assert self.n == self.k, (self.n, self.k)
                self.at, self.n = self.before + turns * self.k, 0

        def group_rows(v):
            return (v[0:HG * GE].rearrange("(g e) -> g e", e=GE),
                    v[HG * GE:(G - 1) * GE].rearrange("(g e) -> g e", e=GE),
                    v[LAST:E].rearrange("(g e) -> g e", e=GE))

        def wait_apart(eng, s, value):
            eng.wait_ge(s, value)
            eng.sem_inc(waited[eng.engine], 1)

        nodes = lambda v: v.rearrange("(p i) d -> p i d", i=NI)

        def scattered_loads(sp, n):
            sums = (sums0, sums1)[n]
            sp.wait_ge(sc["cleared", n], 1)
            sp.dma_start(sums.rearrange("(p r) k -> p (r k)", p=P), acc[:, 0:SROWS // P * KA]).then_inc(sc["zeroed", n], 16)

            def tile(t, first):
                for v, to in ((src, s_src), (dst, s_dst), (edge_type, s_typ)):
                    sp.dma_start(to, v[bass.ds(first, P)].rearrange("(p a) -> p a", a=1)).then_inc(sc["ids", n], 16)
                sp.dma_start(s_attr[:, 0:F], edge_attr[bass.ds(first, P), :]).then_inc(sc["ids", n], 16)

            sp.wait_ge(sc["zeroed", n], 16)
            sp.wait_ge(sc["consts", n], 6)
            tile(0, 0)
            with sp.Fori(1, NT) as t:
                wait_apart(sp, sc["added", n], 16 * t)
                tile(t, t * P)
            sp.wait_ge(sc["added", n], 16 * NT)
            tile(NT, E - P)
            sp.wait_ge(sc["added", n], 16 * (NT + 1))
            with sp.Fori(0, NI) as i:
                wait_apart(sp, sc["back_turned", n], i + 1)
                sp.dma_start(s_back[0:NP, :], sums[0:N, :].rearrange("(p i) k -> p i k", i=NI)[:, bass.ds(i, 1), :].rearrange("p a k -> p (a k)")).then_inc(sc["back_in", n], 16)

        def scattered_gathers(pool, n):
            sums, gathers = (sums0, sums1)[n], (1, 2)[n]
            pool.iota(s_spare_i, pattern=[[0, 1]], base=N, channel_multiplier=1).then_inc(sc["consts", n], 1)
            pool.memset(s_tri, 1.0).then_inc(sc["consts", n], 1)
            pool.memset(s_tail, 1.0).then_inc(sc["consts", n], 1)
            pool.memset(s_attr, 0.0).then_inc(sc["consts", n], 1)
            pool.wait_ge(sc["consts", n], 4)
            pool.affine_select(out=s_tri, in_=s_tri, compare_op=ALU.is_gt, fill=0.0, base=0,
                               pattern=[[-1, P]], channel_multiplier=1).then_inc(sc["consts", n], 1)
            pool.affine_select(out=s_tail, in_=s_tail, compare_op=ALU.is_ge, fill=0.0, base=-(P - (E - NT * P)),
                               pattern=[[0, 1]], channel_multiplier=1).then_inc(sc["consts", n], 1)

            def tile(t):
                wait_apart(pool, sc["ids", n], 64 * (t + 1))
                pool.indirect_dma_start(rows[:, 0, 0, :], None, (h_table, p_table)[n],
                                        bass.IndirectOffsetOnAxis(ap=s_src, axis=0)).then_inc(sc["gathered", n], 16)
                if n == 1:
                    pool.indirect_dma_start(s_q, None, q_table,
                                            bass.IndirectOffsetOnAxis(ap=s_dst, axis=0)).then_inc(sc["gathered", n], 16)
                wait_apart(pool, sc["placed", n], t + 1)
                pool.indirect_dma_start(sums, bass.IndirectOffsetOnAxis(ap=s_out_i, axis=0), s_comb, None,
                                        compute_op=ALU.add).then_inc(sc["added", n], 16)

            with pool.Fori(0, NT) as t:
                tile(t)
            tile(NT)

        def scattered_copies(act, n):
            def tile(t):
                act.wait_ge(sc["turned", n], t + 1)
                if n == 0:
                    act.copy(s_gt[0:D, :], ps[0:D, 1, 0:P]).then_inc(sc["turn_copied", n], 1)
                else:
                    act.copy(attr_t[0:T * F, 0, :], ps[0:T * F, 1, 0:P]).then_inc(sc["turn_copied", n], 1)

            with act.Fori(0, NT) as t:
                tile(t)
            tile(NT)

        def scattered_products(pe, n):
            def tile(t):
                pe.wait_ge(sc["dst_float", n], t + 1)
                pe.matmul(ps[:, 0, 0:P], s_dstf.broadcast_to([P, P]), ident[:], start=True, stop=True)
                if n == 0:
                    wait_apart(pe, sc["gathered", n], 16 * (t + 1))
                    pe.transpose(ps[0:D, 1, 0:P], rows[:, 0, 0, :], ident[:]).then_inc(sc["turned", n], 1)
                    pe.wait_ge(sc["turn_copied", n], t + 1)
                    for half in range(2):
                        r = slice(half * R // 2, (half + 1) * R // 2)
                        last = pe.matmul(ps[:, 2 + half, :], s_gt[0:D, :], w_all[:, r, :].rearrange("k r m -> k (r m)"), start=True, stop=True)
                else:
                    wait_apart(pe, sc["ids", n], 64 * (t + 1))
                    pe.transpose(ps[0:T * F, 1, 0:P], s_attr, ident[:]).then_inc(sc["turned", n], 1)
                    pe.wait_ge(sc["turn_copied", n], t + 1)
                    last = pe.matmul(ps[:, 2, 0:D], attr_t[:, 0, :], w_attr[:, 0, :], start=True, stop=True)
                last.then_inc(sc["made", n], 1)
                pe.wait_ge(sc["masked", n], t + 1)
                pe.matmul(ps[:, 4, 0:KA], s_eq, s_msg, start=True, stop=True).then_inc(sc["summed", n], 1)

            with pe.Fori(0, NT) as t:
                tile(t)
            tile(NT)
            pe.sem_inc(sc["back_turned", n], 1)
            with pe.Fori(0, NI) as i:
                pe.wait_ge(sc["back_in", n], 16 * (i + 1))
                wait_apart(pe, sc["back_copied", n], i + 1)
                pe.transpose(ps[0:KA, 5, 0:NP], s_back[0:NP, :], ident[0:NP, 0:NP]).then_inc(sc["back_turned", n], 1)

        def scattered_sums(dve, n):
            chain = Chain(dve, sc["chain", n])
            dve.sem_inc(sc["cleared", n], 1)
            dve.wait_ge(sc["consts", n], 6)
            chain(dve.tensor_copy(s_spare, s_spare_i))

            def tile(t, valid):
                dve.wait_ge(sc["ids", n], 64 * (t + 1))
                chain(dve.tensor_copy(s_dstf, s_dst))
                dve.sem_inc(sc["dst_float", n], 1)
                dve.wait_ge(sc["turned", n], t + 1)
                chain(dve.tensor_scalar(s_eq, ps[:, 0, 0:P], s_dstf, None, ALU.is_equal))
                chain(dve.tensor_tensor(s_tmp, s_eq, s_tri, ALU.mult))
                chain(dve.tensor_reduce(s_dup, s_tmp, X, ALU.max))
                chain(dve.tensor_tensor(s_row_f, s_spare, s_dstf, ALU.subtract))
                chain(dve.scalar_tensor_tensor(out=s_row_f, in0=s_row_f, scalar=s_dup, in1=s_dstf, op0=ALU.mult, op1=ALU.add))
                chain(dve.tensor_copy(s_out_i, s_row_f))
                dve.wait_ge(sc["made", n], t + 1)
                if n == 0:
                    chain(dve.tensor_copy(s_typf, s_typ))
                    chain(dve.tensor_scalar(s_mask, iota_f[:, 0:R], s_typf, None, ALU.is_equal))
                    both = ps[:, 2:4, :].rearrange("p a b -> p (a b)").rearrange("p (r m) -> p r m", m=D)
                    chain(dve.tensor_tensor(s_prod, both, s_mask.rearrange("p (r a) -> p r a", a=1).broadcast_to([P, R, D]), ALU.mult))
                    chain(dve.tensor_reduce(s_msg[:, 0:D], s_prod.rearrange("p r m -> p m r"), X, ALU.add))
                else:
                    dve.wait_ge(sc["gathered", n], 32 * (t + 1))
                    chain(dve.tensor_tensor(s_pre, ps[:, 2, 0:D], rows[:, 0, 0, :], ALU.add))
                    for part in (2, 1, 0):
                        chain(dve.tensor_tensor(s_pre, s_pre, s_q[:, part * D:(part + 1) * D], ALU.add))
                    chain(dve.tensor_scalar(s_msg[:, 0:D], s_pre, 0.0, None, ALU.max))
                chain(dve.memset(s_msg[:, D:KA], 1.0))
                dve.tensor_scalar(s_msg, s_msg, valid, None, ALU.mult).then_inc(sc["masked", n], 1)
                dve.wait_ge(sc["summed", n], t + 1)
                dve.tensor_copy(s_comb, ps[:, 4, 0:KA]).then_inc(sc["placed", n], 1)

            links = 12 if n == 0 else 13
            with dve.Fori(0, NT) as t:
                chain.enter(t, links)
                tile(t, ones[:])
                chain.leave(NT)
            tile(NT, s_tail)
            dve.sem_inc(sc["back_copied", n], 1)
            with dve.Fori(0, NI) as i:
                dve.wait_ge(sc["back_turned", n], i + 2)
                dve.tensor_copy(acc_nodes[0:KA, bass.ds(i, 1), :].rearrange("k a p -> k (a p)"), ps[0:KA, 5, 0:NP]).then_inc(sc["back_copied", n], 1)
            dve.wait_ge(sc["back_copied", n], NI + 1)

        @block.sync
        def _(sp):
            for v, to, s in ((dst, dst_i, ids_in[0]), (src, src_i, ids_in[1]), (edge_type, typ_i, ids_in[2])):
                first, second, last = group_rows(v)
                sp.dma_start(to[:, 0, :], first).then_inc(s, 16)
                sp.dma_start(to[0:HG - 1, 1, :], second).then_inc(s, 16)
                sp.dma_start(to[HG - 1:HG, 1, :], last).then_inc(s, 16)
            for c in range(NC):
                sp.dma_start(xs[0:NP, c * CI:(c + 1) * CI, :], nodes(x)[:, c * CI:(c + 1) * CI, :]).then_inc(x_in[c], 16)
            sp.dma_start(base_row[0:1, 0:G - 1, :].rearrange("a g t -> a (g t)"),
                         dst[0:(G - 1) * GE].rearrange("(a t p) -> a t p", a=1, p=P)[:, :, 0], allow_slow_non_contiguous=True).then_inc(base_in, 16)
            sp.dma_start(base_row[0:1, G - 1, :],
                         dst[LAST:E].rearrange("(a t p) -> a t p", a=1, p=P)[:, :, 0], allow_slow_non_contiguous=True).then_inc(base_in, 16)
            for c in range(NC):
                sp.wait_ge(h_made, c + 1)
                sp.dma_start(nodes(h_table)[:, c * CI:(c + 1) * CI, :], h[0:NP, c % 2]).then_inc(h_stored[c % 2], 16)

            sp.wait_ge(flag_made, 1)
            fits = sp.value_load(flag[0:1, 0:1], min_val=0, max_val=1)
            with sp.If(fits > 0):
                sp.wait_ge(prep_copied, 4)
                with sp.Fori(0, NIT) as it:
                    for u in range(U):
                        g = it * U + u
                        wait_apart(sp, slots_summed, 2 * (g + 1))
                        sp.dma_start(idx[:, u, :], src_tab[:, bass.ds(g, 1), :]).then_inc(idx0_in[u], 16)
            with sp.Else():
                scattered_loads(sp, 0)

            sp.wait_ge(consts_made, 6)
            sp.dma_start(q_table[N:N + P, :], zrows[:]).then_inc(q_stored, 16)
            sp.sem_inc(chunk_stored, 1)
            with sp.Fori(0, NC) as c:
                wait_apart(sp, pq_copied, 3 + (c + 1) * (CI // SUB))
                sp.dma_start(nodes(p_table)[:, bass.ds(c * CI, CI), :], pq[0:NP, :, 0:D]).then_inc(p_stored, 16)
                wait_apart(sp, q_split, c + 1)
                sp.dma_start(nodes(q_table[0:N, :])[:, bass.ds(c * CI, CI), :],
                             q3[0:NP].rearrange("p i s d -> p i (s d)")).then_inc(q_stored, 16)
                wait_apart(sp, p_stored, 16 * (c + 1))
                wait_apart(sp, q_stored, 16 * (c + 2))
                sp.sem_inc(chunk_stored, 1)

            sp.wait_ge(base_in, 32)
            with sp.If(fits > 0):
                sp.wait_ge(starts_made, 1)
                begin = sp.value_load(start_row[0:1, 0:1], min_val=0, max_val=LAST)
                sp.dma_start(attr[:, 0, :], edge_attr[bass.ds(begin, GE), :].rearrange("(p j) f -> p (j f)", j=T)).then_inc(attr_in[0], 16)
                with sp.Fori(0, NIT) as it:
                    for u in range(U):
                        g = it * U + u
                        begin = sp.value_load(start_row[0:1, bass.ds(g, 1)], min_val=0, max_val=LAST)
                        base = sp.value_load(base_row[0:1, bass.ds(g, 1), 0], min_val=0, max_val=N - 1)
                        after = sp.value_load(start_row[0:1, bass.ds(g + 1, 1)], min_val=0, max_val=LAST)
                        wait_apart(sp, z_made, g + 1)
                        sp.dma_start(idx[:, u, :], src[bass.ds(begin, GE)].rearrange("(p j) -> p j", j=T)).then_inc(idx1_in[u], 16)
                        sp.dma_start(q_win[:, u, :], q_table[bass.ds(base, P), :]).then_inc(q_in[u], 16)
                        wait_apart(sp, group_turned, AHEAD + g - 2)
                        sp.dma_start(attr[:, (u + 1) % U, :],
                                     edge_attr[bass.ds(after, GE), :].rearrange("(p j) f -> p (j f)", j=T)).then_inc(attr_in[(u + 1) % U], 16)
            with sp.Else():
                scattered_loads(sp, 1)

            for c in range(NC):
                sp.wait_ge(out_added, c + 3)
                sp.dma_start(nodes(out)[:, c * CI:(c + 1) * CI, :], xs[0:NP, c * CI:(c + 1) * CI, :]).then_inc(out_stored, 16)
            sp.wait_ge(out_stored, 16 * NC)

        @block.gpsimd
        def _(pool):
            chain = Chain(pool, pool_chain, wait_apart)
            chain(pool.memset(ident[:], 0.0))
            pool.affine_select(out=ident[:], in_=ident[:], compare_op=ALU.not_equal, fill=1.0, base=0,
                               pattern=[[-1, P]], channel_multiplier=1).then_inc(consts_made, 1)
            pool.iota(iota_i[:], pattern=[[1, PAR * C0]], base=0, channel_multiplier=0).then_inc(consts_made, 1)
            pool.iota(start_row[:], pattern=[[1, G + 1]], base=0, channel_multiplier=0).then_inc(consts_made, 1)
            pool.memset(relus[:], 1.0).then_inc(consts_made, 1)
            pool.memset(attr_t[:], 1.0).then_inc(consts_made, 1)
            pool.memset(zrows[:], 0.0).then_inc(consts_made, 1)
            pool.wait_ge(consts_made, 6)
            lo = (HG - 1) // 32 * 32
            for n, key in enumerate((key0_g, key1_g)):
                pool.wait_ge(keys_made, n + 1)
                if n:
                    pool.wait_ge(keys_masked, n)
                v = key[lo:HG, 1, 0:DUP]
                pool.affine_select(out=v, in_=v, compare_op=ALU.not_equal, fill=FAR, base=lo - (HG - 1),
                                   pattern=[[0, DUP]], channel_multiplier=1).then_inc(keys_masked, 1)

            pool.wait_ge(flag_made, 1)
            fits = pool.value_load(flag[0:1, 0:1], min_val=0, max_val=1)
            for b in range(2):
                pool.wait_ge(h_stored[b], 16 * ((NC + 1 - b) // 2))
            with pool.If(fits > 0):
                with pool.Fori(0, NIT) as it:
                    for u in range(U):
                        wait_apart(pool, idx0_in[u], 16 * (it + 1))
                        for t in range(T):
                            pool.indirect_dma_start(rows[:, u, t, :], None, h_table,
                                                    bass.IndirectOffsetOnAxis(ap=idx[:, u, t:t + 1], axis=0)).then_inc(rows0_in[u], 16)
            with pool.Else():
                scattered_gathers(pool, 0)

            pool.wait_ge(layer0_summed, 1)
            pool.tensor_copy(stage_a[0:D], acc_nodes[0:D, 0:CI, :]).then_inc(staged, 1)

            def split_q(c):
                wait_apart(pool, pq_copied, 3 + (c + 1) * (CI // SUB))
                wait_apart(pool, chunk_stored, c + 1)
                q = pq[0:NP, :, D:2 * D]
                chain(pool.tensor_copy(q3[0:NP, :, 0, :], q))
                chain(pool.tensor_tensor(q_rest[0:NP], q, q3[0:NP, :, 0, :], ALU.subtract))
                chain(pool.tensor_copy(q3[0:NP, :, 1, :], q_rest[0:NP]))
                pool.tensor_tensor(q3[0:NP, :, 2, :], q_rest[0:NP], q3[0:NP, :, 1, :], ALU.subtract).then_inc(q_split, 1)

            with pool.Fori(0, NC - 1) as c:
                chain.enter(c, 3)
                wait_apart(pool, turned, c + 1)
                pool.tensor_copy(stage_a[0:D], acc_nodes[0:D, bass.ds(c * CI + CI, CI), :]).then_inc(staged, 1)
                split_q(c)
                chain.leave(NC - 1)
            split_q(NC - 1)

            pool.wait_ge(chunk_stored, NC + 1)
            with pool.If(fits > 0):
                with pool.Fori(0, NIT) as it:
                    for u in range(U):
                        wait_apart(pool, idx1_in[u], 16 * (it + 1))
                        for j in range(T):
                            pool.indirect_dma_start(rows[:, u, j, :], None, p_table,
                                                    bass.IndirectOffsetOnAxis(ap=idx[:, u, j:j + 1], axis=0)).then_inc(rows1_in[u], 16)
            with pool.Else():
                scattered_gathers(pool, 1)

            pool.wait_ge(layer1_summed, 1)
            for c in range(NC):
                if c >= 2:
                    pool.wait_ge(out_made, c - 1)
                stage = (stage_a, stage_b)[c % 2]
                pool.tensor_copy(stage[0:KA], acc_nodes[0:KA, c * CI:(c + 1) * CI, :]).then_inc(out_staged, 1)

        @block.scalar
        def _(act):
            act.wait_ge(blocks_cleared, 1)
            for par in range(PAR):
                act.dma_start(w_pairs[par * D:(par + 1) * D], rel_weight.rearrange("(r a) k m -> a k r m", a=PAR)[par]).then_inc(weights_in, 16)
            act.dma_start(w_all[:], rel_weight.rearrange("r k m -> k r m")).then_inc(weights_in, 16)
            for half in range(2):
                for a in range(2):
                    act.dma_start(w1ab[half * D:(half + 1) * D, half, a * D:(a + 1) * D], w1[a * D:(a + 1) * D, :]).then_inc(weights_in, 16)
            for j in range(T):
                act.dma_start(w_attr[j * F:(j + 1) * F, j, :], w1[2 * D:2 * D + F, :]).then_inc(weights_in, 16)
                act.dma_start(w_attr[T * F:T * F + 1, j, :], b1.rearrange("(a m) -> a m", a=1)).then_inc(weights_in, 16)
            act.dma_start(w2b[0:D, :], w2).then_inc(weights_in, 16)
            act.dma_start(w2b[D:KA, :], b2.rearrange("(a m) -> a m", a=1)).then_inc(weights_in, 16)

            def norm(k):
                act.wait_ge(centered, k + 1)
                act.activation(sq[0:NP], xc[0:NP], ACT.Square).then_inc(squared, 1)
                act.wait_ge(var_made, k + 1)
                act.activation(stat[0:NP, 2, :], stat[0:NP, 1, :], ACT.Sqrt, bias=eps[0:NP, :], scale=1.0 / D).then_inc(std_made, 1)

            act.wait_ge(ids_in[1], 48)
            act.copy(src_f, src_i).then_inc(src_float, 1)
            order = [("table", n) for n in range(4)] + [("norm", k) for k in range(NC)] + [("table", n) for n in range(4, 12)]
            for what, n in order:
                if what == "norm":
                    norm(n)
                    continue
                table, a, half = (src_tab, key0, key1)[n // 4], n // 2 % 2, n % 2
                act.wait_ge(prep_turned, n + 1)
                act.copy(table[:, a * HG:(a + 1) * HG, half * 4:half * 4 + 4].rearrange("p g t -> p t g"),
                         ps[:, n % 4, 0:4 * HG].rearrange("p (t g) -> p t g", g=HG)).then_inc(prep_copied, 1)

            act.sem_inc(pq_copied, 3)
            act.sem_inc(relu_made, AHEAD)
            act.wait_ge(flag_made, 1)
            fits = act.value_load(flag[0:1, 0:1], min_val=0, max_val=1)
            with act.If(fits > 0):
                with act.Fori(0, NIT) as it:
                    for u in range(U):
                        g = it * U + u
                        act.wait_ge(typed, g + 3)
                        for half in range(2):
                            act.wait_ge(slots_summed, 2 * AHEAD + 2 * g + half + 1)
                            t = slice(half * T // 2, (half + 1) * T // 2)
                            act.copy(slots[:, u % 2, t, :], slot_ps[:, u % 2, t, :]).then_inc(slots_copied, 1)

            with act.Else():
                scattered_copies(act, 0)

            with act.Fori(0, NC) as c:
                norm(NC + c)
                act.wait_ge(h_turned, c + 2)
                act.wait_ge(pq_made, c * (CI // SUB) + 1)
                act.copy(h_t, ht_ps[:, :, 0:NP]).then_inc(ht_copied, 1)
                for s in range(CI // SUB):
                    act.wait_ge(pq_made, c * (CI // SUB) + s + 2)
                    if s == 0:
                        act.wait_ge(chunk_stored, c + 1)
                    act.copy(pq[0:NP, s * SUB:(s + 1) * SUB, :].rearrange("p i d -> p (i d)"),
                             pq_ps[:, s % 2, :]).then_inc(pq_copied, 1)

            with act.If(fits > 0):
                def copy_turned(g, b):
                    act.wait_ge(group_turned, AHEAD + g + 1)
                    act.wait_ge(pre_made, g + 3)
                    act.copy(attr_t[0:T * F, b, :], attrt_ps).then_inc(turn_copied, 1)
                    for half in range(2):
                        cols = slice(half * 512, (half + 1) * 512)
                        act.copy(onehot_t[:, b, cols], oht_ps[:, cols]).then_inc(turn_copied, 1)

                copy_turned(0, 0)
                with act.Fori(0, NIT) as it:
                    for u in range(U):
                        g = it * U + u
                        act.wait_ge(pre_added, g + AHEAD + 1)
                        act.wait_ge(z_made, g + 3)
                        act.activation(relus[:, u % 2, :, 0:D], presum[:, u % 2, 0:T * D].rearrange("p (t d) -> p t d", d=D),
                                       ACT.Relu).then_inc(relu_made, 1)
                        copy_turned(g + 1, (u + 1) % 2)
            with act.Else():
                scattered_copies(act, 1)

        @block.vector
        def _(dve):
            chain = Chain(dve, dve_chain)
            dve.memset(ones[:], 1.0)
            dve.memset(eps[:], 1e-5)
            for key in (key0, key1):
                dve.memset(key[:, G, :], FAR)
            dve.memset(w1ab[:], 0.0)
            chain(dve.memset(w_attr[:], 0.0))
            dve.sem_inc(blocks_cleared, 1)

            dve.wait_ge(ids_in[0], 48)
            chain(dve.tensor_copy(dst_f, dst_i))
            dve.wait_ge(ids_in[2], 48)
            chain(dve.tensor_single_scalar(par_i, typ_i, 1, ALU.bitwise_and))
            chain(dve.scalar_tensor_tensor(out=typ_f, in0=par_i, scalar=float((C0 - W0 // PAR) // (W0 // PAR)), in1=typ_i, op0=ALU.mult, op1=ALU.add))
            tiles = lambda v: v.rearrange("g a (t p) -> g (a t) p", p=P)
            chain(dve.tensor_tensor(tiles(off0), tiles(dst_f), tiles(dst_f)[:, :, 0:1].broadcast_to([HG, 2 * T, P]), ALU.subtract))
            dve.scalar_tensor_tensor(out=key0_g, in0=typ_f, scalar=float(W0 // PAR), in1=off0, op0=ALU.mult, op1=ALU.add).then_inc(keys_made, 1)
            chain(dve.tensor_tensor(key1_g, dst_f, dst_f[:, :, 0:1].broadcast_to([HG, 2, GE]), ALU.subtract))
            e = extremes
            dve.tensor_reduce(e[0:HG, 0:1], off0, mybir.AxisListType.XY, ALU.max)
            dve.tensor_reduce(e[0:HG, 1:2], off0, mybir.AxisListType.XY, ALU.min)
            heads = tiles(key1_g)[:, :, 0]
            dve.tensor_reduce(e[0:HG, 2:3], heads[:, 0:2 * T - T], X, ALU.max)
            chain(dve.tensor_reduce(e[0:HG, 3:4], heads, X, ALU.min))
            dve.sem_inc(keys_made, 1)

            bad = e[0:HG, 4:5]
            chain(dve.tensor_scalar(bad, e[0:HG, 0:1], float(W0), None, ALU.is_ge))
            for col, op, limit in ((1, ALU.is_lt, 0.0), (2, ALU.is_gt, float(W1N - W0)), (3, ALU.is_lt, 0.0)):
                chain(dve.scalar_tensor_tensor(out=bad, in0=e[0:HG, col:col + 1], scalar=limit, in1=bad, op0=op, op1=ALU.add))
            dve.sem_inc(bad_made, 1)
            dve.wait_ge(consts_made, 6)
            dve.tensor_copy(iota_f[:], iota_i[:])
            chain(dve.tensor_scalar(start_row[:], start_row[:], float(GE), float(LAST), ALU.mult, ALU.min))
            dve.sem_inc(starts_made, 1)

            def norm(xv, hv, k, free=None):
                s1, var, std, rstd = (stat[0:NP, n, :] for n in range(4))
                wide = lambda v: v.rearrange("p (i a) -> p i a", a=1).broadcast_to([NP, CI, D])
                chain(dve.tensor_reduce(s1, xv, X, ALU.add))
                dve.scalar_tensor_tensor(out=xc[0:NP], in0=wide(s1), scalar=-1.0 / D, in1=xv, op0=ALU.mult, op1=ALU.add).then_inc(centered, 1)
                dve.wait_ge(squared, k + 1)
                dve.tensor_reduce(var, sq[0:NP], X, ALU.add).then_inc(var_made, 1)
                dve.wait_ge(std_made, k + 1)
                chain(dve.reciprocal(rstd, std))
                if free is not None:
                    free()
                dve.wait_ge(centered, k + 1)
                dve.scalar_tensor_tensor(out=hv, in0=xc[0:NP], scalar=0.0, in1=wide(rstd), op0=ALU.max, op1=ALU.mult).then_inc(h_made, 1)

            for c in range(NC):
                dve.wait_ge(x_in[c], 16)
                def h_free():
                    if c >= 2:
                        dve.wait_ge(h_stored[c % 2], 16 * (c // 2))
                norm(xs[0:NP, c * CI:(c + 1) * CI, :], h[0:NP, c % 2], c, h_free)
                if c == 0:
                    dve.wait_ge(bad_summed, 1)
                    dve.tensor_scalar(flag[:], ps[0:1, 4, 0:1], 0.5, None, ALU.is_lt).then_inc(flag_made, 1)

            dve.wait_ge(prep_turned, 12)
            dve.sem_inc(x_added, 1)
            dve.sem_inc(out_added, 2)
            dve.wait_ge(flag_made, 1)
            fits = dve.value_load(flag[0:1, 0:1], min_val=0, max_val=1)
            chain(dve.memset(acc[:], 0.0))
            with dve.If(fits > 0):
                dve.sem_inc(window_added, AHEAD * T)
                dve.wait_ge(prep_copied, 12)
                dve.wait_ge(base_in, 32)

                def make_onehot0(g, b):
                    dve.wait_ge(slots_summed, 2 * AHEAD + 2 * g - 2)
                    dve.tensor_tensor(onehot[:, b], key0[:, bass.ds(g, 1), :].rearrange("p a (t c) -> p (a t) c", c=1).broadcast_to([P, T, PAR * C0]),
                                      iota_f[:].rearrange("p (a c) -> p a c", a=1).broadcast_to([P, T, PAR * C0]), ALU.is_equal).then_inc(onehot0, 1)

                make_onehot0(0, 0)
                with dve.Fori(0, NIT) as it:
                    for u in range(U):
                        g = it * U + u
                        make_onehot0(g + 1, (u + 1) % 2)
                        _, bases = nc.values_load_multi_w_load_instructions(
                            base_row[0:1, bass.ds(g, 1), :].rearrange("a g t -> a (g t)"), engines=[ENG.DVE], min_val=0, max_val=N - 1,
                            skip_runtime_bounds_check_because="dst holds nodes' numbers")
                        dve.wait_ge(typed, AHEAD + g + 1)
                        for t in range(T):
                            window = acc[0:D, bass.ds(bases[t], W0)]
                            dve.wait_ge(window_added, AHEAD * T + g * T + t)
                            dve.tensor_tensor(window, window, node_ps[:, u % 2, t * W0:(t + 1) * W0], ALU.add).then_inc(window_added, 1)
                dve.wait_ge(window_added, (AHEAD + G) * T)
            with dve.Else():
                scattered_sums(dve, 0)
            dve.sem_inc(layer0_summed, 1)

            with dve.Fori(0, NC) as c:
                chain.enter(c, 2)
                xv = xs[0:NP, bass.ds(c * CI, CI), :]
                dve.wait_ge(turned, c + 1)
                dve.tensor_tensor(xv, xv, x_ps.rearrange("p (i d) -> p i d", d=D), ALU.add).then_inc(x_added, 1)
                wait_apart(dve, x_added, c + 2)
                norm(xv, h[0:NP, 0], NC + c, lambda: dve.wait_ge(h_turned, c + 1))
                chain.leave(NC)

            dve.wait_ge(pq_made, 1 + NI // SUB)
            chain(dve.memset(acc[:], 0.0))
            with dve.If(fits > 0):
                dve.sem_inc(pre_added, AHEAD)
                dve.sem_inc(z_added, AHEAD)
                oh1 = onehot[:, :, :, 0:P]

                def make_onehot1(g, b):
                    dve.wait_ge(z_made, AHEAD + g - 1)
                    dve.tensor_tensor(oh1[:, b], key1[:, bass.ds(g, 1), :].rearrange("p a (t c) -> p (a t) c", c=1).broadcast_to([P, T, P]),
                                      iota_f[:, 0:P].rearrange("p (a c) -> p a c", a=1).broadcast_to([P, T, P]), ALU.is_equal).then_inc(onehot1, 1)

                make_onehot1(0, 0)
                with dve.Fori(0, NIT) as it:
                    _, bases = nc.values_load_multi_w_load_instructions(
                        base_row[0:1, bass.ds(it * U, U), 0], engines=[ENG.DVE], min_val=0, max_val=N - 1,
                        skip_runtime_bounds_check_because="dst holds nodes' numbers")
                    for u in range(U):
                        g, b = it * U + u, u % 2
                        make_onehot1(g + 1, (u + 1) % 2)
                        dve.wait_ge(pre_made, AHEAD + g + 1)
                        dve.wait_ge(rows1_in[u], 16 * T * (it + 1))
                        dve.wait_ge(relu_made, g + AHEAD - 1)
                        dve.tensor_tensor(presum[:, b, 0:T * D], pre_ps[:, b, :], rows[:, u].rearrange("p t d -> p (t d)"), ALU.add).then_inc(pre_added, 1)
                        dve.wait_ge(z_made, AHEAD + g + 1)
                        window = acc[0:KA, bass.ds(bases[u], W1N)]
                        dve.wait_ge(z_added, AHEAD + g)
                        dve.tensor_tensor(window, window, z_ps[:, b, 0:W1N], ALU.add).then_inc(z_added, 1)
                dve.wait_ge(z_added, AHEAD + G)
            with dve.Else():
                scattered_sums(dve, 1)
            dve.sem_inc(layer1_summed, 1)

            for c in range(NC):
                dve.wait_ge(out_made, c + 1)
                xv = xs[0:NP, c * CI:(c + 1) * CI, :].rearrange("p i d -> p (i d)")
                dve.tensor_tensor(xv, xv, out_ps[c % 2], ALU.add).then_inc(out_added, 1)

        @block.tensor
        def _(pe):
            for s, n in ((slots_summed, 2 * AHEAD), (typed, AHEAD), (pre_made, AHEAD), (z_made, AHEAD), (pq_made, 1), (h_turned, 1), (group_turned, AHEAD)):
                pe.sem_inc(s, n)
            pe.wait_ge(consts_made, 1)
            for n in range(12):
                v = (src_f, key0_g, key1_g)[n // 4][:, n // 2 % 2, :]
                v = v.rearrange("g (p j) -> g j p", j=T) if n >= 8 else v.rearrange("g (t p) -> g t p", p=P)
                if n == 0:
                    pe.wait_ge(src_float, 1)
                elif n % 4 == 0:
                    pe.wait_ge(keys_masked, n // 4)
                if n == 8:
                    pe.wait_ge(bad_made, 1)
                    pe.matmul(ps[0:1, 4, 0:1], extremes[0:HG, 4:5], ones[0:HG, :], start=True, stop=True).then_inc(bad_summed, 1)
                if n >= 4:
                    pe.wait_ge(prep_copied, n - 3)
                for t in range(4):
                    last = pe.transpose(ps[:, n % 4, t * HG:(t + 1) * HG], v[:, n % 2 * 4 + t, :], ident[0:HG, 0:HG])
                last.then_inc(prep_turned, 1)

            pe.wait_ge(flag_made, 1)
            fits = pe.value_load(flag[0:1, 0:1], min_val=0, max_val=1)
            pe.wait_ge(prep_copied, 12)
            pe.wait_ge(weights_in, 16 * (PAR + 1 + 4 + 2 * T + 2))
            with pe.If(fits > 0):
                with pe.Fori(0, NIT) as it:
                    for u in range(U):
                        g, b = it * U + u, u % 2
                        pe.wait_ge(onehot0, g + 1)
                        pe.wait_ge(rows0_in[u], 16 * T * (it + 1))
                        for t in range(T):
                            for par in range(PAR):
                                last = pe.matmul(slot_ps[par * D:(par + 1) * D, b, t, :], rows[:, u, t, :],
                                                 onehot[:, b, t, par * C0:(par + 1) * C0], start=True, stop=True)
                            if t % 4 == 3:
                                last.then_inc(slots_summed, 1)
                        pe.wait_ge(slots_copied, 2 * (g + 1))
                        pe.wait_ge(window_added, T * (g + AHEAD - 1))
                        for r in range(RP):
                            last = pe.matmul(node_ps[:, b, 0:T * W0], w_pairs[:, r, :], slots[:, b, :, r * W0:(r + 1) * W0],
                                             start=(r == 0), stop=(r == RP - 1))
                        last.then_inc(typed, 1)
            with pe.Else():
                scattered_products(pe, 0)

            with pe.Fori(0, NC) as c:
                pe.wait_ge(staged, c + 1)
                wait_apart(pe, x_added, c + 1)
                for i in range(CI):
                    last = pe.transpose(x_ps[:, i * D:(i + 1) * D], stage_a[0:D, i, :], ident[0:D, 0:D])
                last.then_inc(turned, 1)
                wait_apart(pe, h_made, NC + c + 1)
                for i in range(CI // 2):
                    last = pe.transpose(ht_ps[:, i, 0:NP], h[0:NP, 0, 2 * i:2 * i + 2, :].rearrange("p i d -> p (i d)"), ident[0:NP, 0:NP])
                last.then_inc(h_turned, 1)
                pe.wait_ge(ht_copied, c + 1)
                for s in range(CI // SUB):
                    pe.wait_ge(pq_copied, c * (CI // SUB) + max(s + 2, 3))
                    for i in range(SUB // 2):
                        last = pe.matmul(pq_ps[:, s % 2, i * 4 * D:(i + 1) * 4 * D], h_t[:, s * SUB // 2 + i, :],
                                         w1ab[:].rearrange("k a n -> k (a n)"), start=True, stop=True)
                    last.then_inc(pq_made, 1)

            pe.wait_ge(pq_copied, 3 + NI // SUB)
            pe.wait_ge(x_added, NC + 1)
            with pe.If(fits > 0):
                def turn_group(g, b, at):
                    pe.wait_ge(attr_in[at[0]], 16 * at[1])
                    wait_apart(pe, onehot1, g + 1)
                    pe.transpose(attrt_ps, attr[:, at[0], :], ident[:])
                    for j in range(T):
                        last = pe.transpose(oht_ps[:, j * P:(j + 1) * P], onehot[:, b, j, 0:P], ident[:])
                    last.then_inc(group_turned, 1)

                turn_group(0, 0, (0, 1))
                with pe.Fori(0, NIT) as it:
                    for u in range(U):
                        g, b = it * U + u, u % 2
                        pe.wait_ge(turn_copied, 3 * (g + 1))
                        pe.wait_ge(q_in[u], 16 * (it + 1))
                        pe.wait_ge(pre_added, g + AHEAD - 1)
                        pe.matmul(pre_ps[:, b, :], attr_t[:, b, :], w_attr[:].rearrange("k j d -> k (j d)"), start=True, stop=False)
                        for j in range(T):
                            for part in range(3):
                                last = pe.matmul(pre_ps[:, b, j * D:(j + 1) * D], onehot_t[:, b, j * P:(j + 1) * P],
                                                 q_win[:, u, part * D:(part + 1) * D], start=False, stop=(j == T - 1 and part == 2))
                        last.then_inc(pre_made, 1)
                        turn_group(g + 1, (u + 1) % 2, ((u + 1) % U, it + 1 + (u + 1) // U))
                        pe.wait_ge(relu_made, AHEAD + g + 1)
                        pe.wait_ge(z_added, g + AHEAD - 1)
                        for j in range(T):
                            last = pe.matmul(z_ps[:, b, 0:W1N], relus[:, b, j, :], onehot[:, b, j, 0:P], start=(j == 0), stop=(j == T - 1))
                        last.then_inc(z_made, 1)
                pe.wait_ge(turn_copied, 3 * (G + 1))
            with pe.Else():
                scattered_products(pe, 1)

            def out_chunk(c, b):
                pe.wait_ge(out_staged, c + 1)
                pe.wait_ge(out_added, c + 1)
                for i in range(CI):
                    last = pe.matmul(out_ps[b][:, i * D:(i + 1) * D], (stage_a, stage_b)[b][0:KA, i, :], w2b[:], start=True, stop=True)
                last.then_inc(out_made, 1)

            with pe.Fori(0, NC // 2) as it:
                for b in range(2):
                    out_chunk(it * 2 + b, b)
            out_chunk(NC - 1, 0)


_INS = ['x', 'src', 'dst', 'edge_attr_8', 'edge_type_16', 'L0_gnn_weight', 'L1_gnn_W1', 'L1_gnn_b1', 'L1_gnn_W2', 'L1_gnn_b2']


def kernel(**inputs):
    import numpy as _np
    import concourse.bacc as _bacc
    from concourse import mybir as _mybir
    from concourse.bass_utils import run_bass_kernel_spmd as _run

    nc = _bacc.Bacc("TRN2", target_bir_lowering=False, num_devices=1)
    arrays, args = {}, []
    for name in _INS:
        a = _np.ascontiguousarray(inputs[name])
        arrays[f"in_{name}_dram"] = a
        args.append(nc.dram_tensor(f"in_{name}_dram", a.shape, _mybir.dt.from_np(a.dtype), kind="ExternalInput").ap())
    shape = inputs["x"].shape
    args.append(nc.dram_tensor("out_0_dram", shape, _mybir.dt.float32, kind="ExternalOutput").ap())
    gnn_kernel(nc, *args)
    r = _run(nc, [arrays], core_ids=[0])
    return r.results[0]["out_0_dram"]
```

```python
import concourse.bass as bass
import concourse.mybir as mybir
from concourse.alu_op_type import AluOpType as ALU
from contextlib import ExitStack


def gnn_kernel(nc, x, src, dst, edge_attr, edge_type, rel_weight, w1, b1, w2, b2, out):
    fp32, bf16, i32 = mybir.dt.float32, mybir.dt.bfloat16, mybir.dt.int32
    ACT = mybir.ActivationFunctionType
    X = mybir.AxisListType.X
    ENG = mybir.EngineType

    P = 128
    N, D = x.shape
    E, F = edge_attr.shape
    R = rel_weight.shape[0]
    PAR = 2
    RP = R // PAR
    T = 8
    GE = T * P
    G = -(-E // GE)
    LAST = E - GE
    DUP = GE * (G - 1) - LAST
    HG = G // 2
    U = 4
    NIT = G // U
    W0 = 16
    W1N = P
    C0 = RP * W0
    NSEG = 13
    SEG = NIT // NSEG
    CP, CI = 120, 8
    CN = CP * CI
    NC = NSEG - 1
    LP, LI = 98, 10
    LN0 = NC * CN
    NCOL = NC * CI + LI
    AC = 2
    NA = NC // AC + 1
    KA = D + 1
    ACCN = N + P
    BP = 125
    NT = E // P
    AHEAD = 4
    FAR = float(1 << 20)
    assert G % U == 0 and G % 2 == 0 and LN0 + LP * LI == N and 0 < DUP and NIT == NSEG * SEG and SEG % 2 == 0

    ctx = ExitStack()
    with ctx:
        def sb(name, shape, dt):
            return ctx.enter_context(nc.sbuf_tensor(name, shape, dt))

        def sem(name):
            return ctx.enter_context(nc.semaphore(name))

        def dram(name, shape, dt):
            return nc.dram_tensor(name, shape, dt, kind="Internal").ap()

        h_table = dram("h_table", (N, D), fp32)
        p_table = dram("p_table", (N, D), fp32)
        q_table = dram("q_table", (N + P, 3 * D), bf16)
        SROWS = P * (-(-(N + P) // P))
        sums0 = dram("sums0", (SROWS, KA), fp32)
        sums1 = dram("sums1", (SROWS, KA), fp32)

        acc = sb("acc", [P, ACCN], fp32)
        xs = sb("xs", [P, NCOL, D], fp32)
        src_tab = sb("src_tab", [P, G, T], i32)
        key0 = sb("key0", [P, G + 1, T], fp32)
        key1 = sb("key1", [P, G + 1, T], fp32)
        base_row = sb("base_row", [1, G, T], i32)
        start_row = sb("start_row", [1, G + 1], i32)
        idx = sb("idx", [P, U, T], i32)
        rows = sb("rows", [P, U, T, D], fp32)
        onehot = sb("onehot", [P, 2, T, PAR * C0], fp32)
        slots = sb("slots", [P, 2, T, C0], fp32)
        relus = sb("relus", [P, 2, T, KA], fp32)
        onehot_t = sb("onehot_t", [P, 2, T * P], bf16)
        attr = sb("attr", [P, U, T * F], fp32)
        attr_t = sb("attr_t", [T * F + 1, 2, P], fp32)
        q_win = sb("q_win", [P, U, 3 * D], bf16)
        stage = sb("stage", [P, LP * LI], fp32)
        xc = sb("xc", [P, LI, D], fp32)
        sq = sb("sq", [P, LI, D], fp32)
        h = sb("h", [P, LI, D], fp32)
        h_t = sb("h_t", [P, LI // 2, CP], fp32)
        p_out = sb("p_out", [P, LI, D], fp32)
        q_rest = sb("q_rest", [P, LI, D], fp32)
        q3 = sb("q3", [P, LI, 3, D], bf16)
        stat = sb("stat", [P, 4, LI], fp32)
        stat_a = sb("stat_a", [P, NA, 4, AC * CI], fp32)
        ident = sb("ident", [P, P], fp32)
        iota_i = sb("iota_i", [P, PAR * C0], i32)
        iota_f = sb("iota_f", [P, PAR * C0], fp32)
        ones = sb("ones", [P, 1], fp32)
        eps = sb("eps", [P, 1], fp32)
        zrows = sb("zrows", [P, 3 * D], bf16)
        w_pairs = sb("w_pairs", [P, RP, D], fp32)
        w_all = sb("w_all", [D, R, D], fp32)
        w_attr = sb("w_attr", [T * F + 1, T, D], fp32)
        again = sb("again", [P, DUP], fp32)
        limit_i = sb("limit_i", [HG, 2], i32)
        limit = sb("limit", [HG, 2], fp32)
        w1ab = sb("w1ab", [P, 2, 2 * D], fp32)
        w2b = sb("w2b", [KA, D], fp32)
        extremes = sb("extremes", [P, 6], fp32)
        flag = sb("flag", [1, 1], i32)

        def edge_list(n, dt):
            v = acc[0:HG, n * 2 * GE:(n + 1) * 2 * GE]
            return (v.bitcast(i32) if dt == i32 else v).rearrange("g (a e) -> g a e", a=2)
        dst_i, src_i, typ_i = edge_list(0, i32), edge_list(1, i32), edge_list(2, i32)
        off0, par_i, typ_f = edge_list(3, i32), edge_list(4, i32), edge_list(5, fp32)
        src_f, key0_g, key1_g = edge_list(1, fp32), edge_list(4, fp32), edge_list(2, fp32)

        flat_oh = onehot[:].rearrange("p a b c -> p (a b c)")
        PW = AC * CI
        ring = lambda v, n: v[:, n * PW * D:(n + 1) * PW * D].rearrange("p (i d) -> p i d", d=D)
        xc_a = [ring(flat_oh, n) for n in range(4)]
        sq_a = [ring(slots[:].rearrange("p b t c -> p (b t c)"), n) for n in range(2)]
        h_a = [ring(rows[:].rearrange("p u t d -> p (u t d)"), n) for n in range(2)]
        presum = slots[:].rearrange("p b t c -> p b (t c)")

        s_row = slots[:].rearrange("p b t c -> p (b t c)")
        s_prod = s_row[:, 0:R * D].rearrange("p (r m) -> p r m", m=D)
        s_eq, s_tri, s_tmp = flat_oh[:, 0:P], flat_oh[:, P:2 * P], flat_oh[:, 2 * P:3 * P]
        s_gt = flat_oh[:, 3 * P:4 * P]
        s_msg = flat_oh[:, 4 * P:4 * P + KA]
        s_comb = flat_oh[:, 5 * P:5 * P + KA]
        s_dstf, s_typf = flat_oh[:, 6 * P:6 * P + 1], flat_oh[:, 6 * P + 1:6 * P + 2]
        s_dup, s_row_f = flat_oh[:, 6 * P + 2:6 * P + 3], flat_oh[:, 6 * P + 3:6 * P + 4]
        s_spare, s_tail = flat_oh[:, 6 * P + 4:6 * P + 5], flat_oh[:, 6 * P + 5:6 * P + 6]
        s_mask = flat_oh[:, 6 * P + 8:6 * P + 8 + R]
        s_attr = flat_oh[:, 7 * P:7 * P + T * F]
        s_back = flat_oh[:, 9 * P:9 * P + KA]
        s_pre = flat_oh[:, 10 * P:10 * P + D]
        s_spare_i = idx[:, 0, 4:5]
        s_src, s_dst, s_typ, s_out_i = idx[:, 0, 0:1], idx[:, 0, 1:2], idx[:, 0, 2:3], idx[:, 0, 3:4]
        s_q = q_win[:, 0, :]

        ps = ctx.enter_context(nc.psum_tensor("ps", [P, 8, 512], fp32))
        ps_all = ps[:].rearrange("p a b -> p (a b)")
        slot_ps = ps_all[:, 0:4 * 512].rearrange("p (b t c) -> p b t c", b=2, t=T)
        node_ps = ps_all[0:D, 4 * 512:6 * 512].rearrange("k (b n) -> k b n", b=2)
        oht_ps = ps_all[:, 0:2 * 512]
        attrt_ps = ps[0:T * F, 2, 0:P]
        pre_ps = ps_all[:, 3 * 512:5 * 512].rearrange("p (b c) -> p b c", b=2)
        z_ps = ps_all[0:KA, 5 * 512:7 * 512].rearrange("k (b n) -> k b n", b=2)

        class Nodes:

            def __init__(self, p, n, x_bank, ht_bank, pq_bank, out_bank):
                self.p, self.n = p, n
                at = lambda bank, w: ps_all[:, bank * 512:bank * 512 + w]
                self.x = at(x_bank, n * D)[0:p].rearrange("p (i d) -> p i d", d=D)
                self.ht = at(ht_bank, n // 2 * P).rearrange("k (i p) -> k i p", p=P)[:, :, 0:p]
                self.pq = at(pq_bank, n * 2 * D)[0:p].rearrange("p (i a d) -> p i a d", a=2, d=D)
                self.out = at(out_bank, n * D)[0:p].rearrange("p (i d) -> p i d", d=D)
                self.stage = stage[:, 0:p * n].rearrange("k (p i) -> k i p", i=n)

        chunk_nodes, last_nodes = Nodes(CP, CI, 6, 7, 6, 7), Nodes(LP, LI, 0, 2, 4, 0)

        ids_in = [sem(f"ids_in_{k}") for k in range(3)]
        x_in = [sem(f"x_in_{k}") for k in range(NA)]
        weights_in = sem("weights_in")
        base_in = sem("base_in")
        consts_made = sem("consts_made")
        pool_chain = sem("pool_chain")
        dve_chain = sem("dve_chain")
        starts_made = sem("starts_made")
        src_float = sem("src_float")
        offsets_made = sem("offsets_made")
        keys_made = sem("keys_made")
        bad_made = sem("bad_made")
        bad_summed = sem("bad_summed")
        flag_made = sem("flag_made")
        prep_turned = sem("prep_turned")
        prep_copied = sem("prep_copied")
        centered_a = sem("centered_a")
        squared_a = sem("squared_a")
        var_made_a = sem("var_made_a")
        std_made_a = sem("std_made_a")
        rstd_made_a = sem("rstd_made_a")
        scaled_a = sem("scaled_a")
        h_made_a = sem("h_made_a")
        h_stored = [sem(f"h_stored_{b}") for b in range(2)]
        blocks_cleared = sem("blocks_cleared")
        idx0_in = [sem(f"idx0_in_{u}") for u in range(U)]
        rows0_in = [sem(f"rows0_in_{u}") for u in range(U)]
        onehot0 = sem("onehot0")
        slots_summed = sem("slots_summed")
        slots_copied = sem("slots_copied")
        typed = sem("typed")
        window_added = sem("window_added")
        layer0_summed = sem("layer0_summed")
        staged = sem("staged")
        turned = sem("turned")
        x_added = sem("x_added")
        x_added_sum = sem("x_added_sum")
        rstd_made = sem("rstd_made")
        centered = sem("centered")
        squared = sem("squared")
        var_made = sem("var_made")
        std_made = sem("std_made")
        h_made = sem("h_made")
        h_turned = sem("h_turned")
        ht_copied = sem("ht_copied")
        pq_made = sem("pq_made")
        pq_copied = sem("pq_copied")
        rest_made = sem("rest_made")
        part2_made = sem("part2_made")
        q_split = sem("q_split")
        p_stored = sem("p_stored")
        q_stored = sem("q_stored")
        chunk_stored = sem("chunk_stored")
        idx1_in = [sem(f"idx1_in_{u}") for u in range(U)]
        q_in = [sem(f"q_in_{u}") for u in range(U)]
        attr_in = [sem(f"attr_in_{u}") for u in range(U)]
        rows1_in = [sem(f"rows1_in_{u}") for u in range(U)]
        onehot1 = sem("onehot1")
        group_turned = sem("group_turned")
        turn_copied = sem("turn_copied")
        pre_made = sem("pre_made")
        pre_added = sem("pre_added")
        relu_made = sem("relu_made")
        z_made = sem("z_made")
        z_added = sem("z_added")
        layer1_summed = sem("layer1_summed")
        out_staged = sem("out_staged")
        out_made = sem("out_made")
        out_added = sem("out_added")
        out_stored = sem("out_stored")
        sc = {(k, n): sem(f"scattered{n}_{k}") for n in range(2)
              for k in ("consts", "cleared", "zeroed", "ids", "gathered", "dst_float", "turned", "turn_copied", "made",
                        "masked", "summed", "placed", "added", "back_in", "back_turned", "back_copied", "chain")}

        waited = {e: sem(f"waited_{n}") for e, n in ((ENG.SP, "sync"), (ENG.Pool, "gpsimd"), (ENG.DVE, "vector"), (ENG.PE, "tensor"))}

        block = ctx.enter_context(nc.Block())

        class Chain:

            def __init__(self, eng, s, wait=None):
                self.eng, self.s, self.at, self.n = eng, s, 0, 0
                self.wait = wait or (lambda eng, s, value: eng.wait_ge(s, value))

            def __call__(self, ins):
                self.n += 1
                ins.then_inc(self.s, 1)
                self.wait(self.eng, self.s, self.at + self.n)

            def enter(self, i, k):
                self.before = self.at + self.n
                self.at, self.n, self.k = self.before + i * k, 0, k

            def leave(self, turns):
                assert self.n == self.k, (self.n, self.k)
                self.at, self.n = self.before + turns * self.k, 0

        def group_rows(v):
            return (v[0:HG * GE].rearrange("(g e) -> g e", e=GE),
                    v[HG * GE:(G - 1) * GE].rearrange("(g e) -> g e", e=GE),
                    v[LAST:E].rearrange("(g e) -> g e", e=GE))

        def wait_apart(eng, s, value):
            eng.wait_ge(s, value)
            eng.sem_inc(waited[eng.engine], 1)

        def node_rows(v, c):
            if isinstance(c, int) and c == NC:
                return v[LN0:N, :].rearrange("(p i) d -> p i d", i=LI)
            return v[0:LN0, :].rearrange("(c p i) d -> c p i d", p=CP, i=CI)[bass.ds(c, 1)].rearrange("c p i d -> p (c i) d")

        def piece(k):
            if k == NA - 1:
                return LP, slice(NC * CI, NCOL), lambda v: node_rows(v, NC)
            rows_of = lambda v: v[k * AC * CN:(k + 1) * AC * CN, :].rearrange("(c p i) d -> p c i d", p=CP, i=CI)
            return CP, slice(k * AC * CI, (k + 1) * AC * CI), rows_of

        def by_chunk(v, k):
            return v if k == NA - 1 else v.rearrange("p (c i) d -> p c i d", i=CI)

        def segments(eng, group_body, chunk, at_end=False):
            def iterations(first, n):
                with eng.Fori(first, first + n) as it:
                    for u in range(U):
                        group_body(it, u)
            iterations(0, SEG)
            with eng.Fori(1, NSEG) as s:
                with eng.Fori(0, SEG // 2) as i:
                    for u in range(U):
                        group_body(s * SEG + i, u)
                if not at_end:
                    chunk(s - 1, chunk_nodes)
                with eng.Fori(SEG // 2, SEG) as i:
                    for u in range(U):
                        group_body(s * SEG + i, u)
                if at_end:
                    chunk(s - 1, chunk_nodes)

        def all_chunks(eng, chunk):
            with eng.Fori(0, NC) as c:
                chunk(c, chunk_nodes)

        def scattered_loads(sp, n):
            sums = (sums0, sums1)[n]
            sp.wait_ge(sc["cleared", n], 1)
            sp.dma_start(sums.rearrange("(p r) k -> p (r k)", p=P), acc[:, 0:SROWS // P * KA]).then_inc(sc["zeroed", n], 16)

            def tile(t, first):
                for v, to in ((src, s_src), (dst, s_dst), (edge_type, s_typ)):
                    sp.dma_start(to, v[bass.ds(first, P)].rearrange("(p a) -> p a", a=1)).then_inc(sc["ids", n], 16)
                sp.dma_start(s_attr[:, 0:F], edge_attr[bass.ds(first, P), :]).then_inc(sc["ids", n], 16)

            sp.wait_ge(sc["zeroed", n], 16)
            sp.wait_ge(sc["consts", n], 6)
            tile(0, 0)
            with sp.Fori(1, NT) as t:
                wait_apart(sp, sc["added", n], 16 * t)
                tile(t, t * P)
            sp.wait_ge(sc["added", n], 16 * NT)
            tile(NT, E - P)
            sp.wait_ge(sc["added", n], 16 * (NT + 1))
            with sp.Fori(0, N // BP) as i:
                wait_apart(sp, sc["back_turned", n], i + 1)
                sp.dma_start(s_back[0:BP, :], sums[bass.ds(i * BP, BP), :]).then_inc(sc["back_in", n], 16)

        def scattered_gathers(pool, n):
            sums, gathers = (sums0, sums1)[n], (1, 2)[n]
            pool.iota(s_spare_i, pattern=[[0, 1]], base=N, channel_multiplier=1).then_inc(sc["consts", n], 1)
            pool.memset(s_tri, 1.0).then_inc(sc["consts", n], 1)
            pool.memset(s_tail, 1.0).then_inc(sc["consts", n], 1)
            pool.memset(s_attr, 0.0).then_inc(sc["consts", n], 1)
            pool.wait_ge(sc["consts", n], 4)
            pool.affine_select(out=s_tri, in_=s_tri, compare_op=ALU.is_gt, fill=0.0, base=0,
                               pattern=[[-1, P]], channel_multiplier=1).then_inc(sc["consts", n], 1)
            pool.affine_select(out=s_tail, in_=s_tail, compare_op=ALU.is_ge, fill=0.0, base=-(P - (E - NT * P)),
                               pattern=[[0, 1]], channel_multiplier=1).then_inc(sc["consts", n], 1)

            def tile(t):
                wait_apart(pool, sc["ids", n], 64 * (t + 1))
                pool.indirect_dma_start(rows[:, 0, 0, :], None, (h_table, p_table)[n],
                                        bass.IndirectOffsetOnAxis(ap=s_src, axis=0)).then_inc(sc["gathered", n], 16)
                if n == 1:
                    pool.indirect_dma_start(s_q, None, q_table,
                                            bass.IndirectOffsetOnAxis(ap=s_dst, axis=0)).then_inc(sc["gathered", n], 16)
                wait_apart(pool, sc["placed", n], t + 1)
                pool.indirect_dma_start(sums, bass.IndirectOffsetOnAxis(ap=s_out_i, axis=0), s_comb, None,
                                        compute_op=ALU.add).then_inc(sc["added", n], 16)

            with pool.Fori(0, NT) as t:
                tile(t)
            tile(NT)

        def scattered_copies(act, n):
            def tile(t):
                act.wait_ge(sc["turned", n], t + 1)
                if n == 0:
                    act.copy(s_gt[0:D, :], ps[0:D, 1, 0:P]).then_inc(sc["turn_copied", n], 1)
                else:
                    act.copy(attr_t[0:T * F, 0, :], ps[0:T * F, 1, 0:P]).then_inc(sc["turn_copied", n], 1)

            with act.Fori(0, NT) as t:
                tile(t)
            tile(NT)

        def scattered_products(pe, n):
            def tile(t):
                pe.wait_ge(sc["dst_float", n], t + 1)
                pe.matmul(ps[:, 0, 0:P], s_dstf.broadcast_to([P, P]), ident[:], start=True, stop=True)
                if n == 0:
                    wait_apart(pe, sc["gathered", n], 16 * (t + 1))
                    pe.transpose(ps[0:D, 1, 0:P], rows[:, 0, 0, :], ident[:]).then_inc(sc["turned", n], 1)
                    pe.wait_ge(sc["turn_copied", n], t + 1)
                    for half in range(2):
                        r = slice(half * R // 2, (half + 1) * R // 2)
                        last = pe.matmul(ps[:, 2 + half, :], s_gt[0:D, :], w_all[:, r, :].rearrange("k r m -> k (r m)"), start=True, stop=True)
                else:
                    wait_apart(pe, sc["ids", n], 64 * (t + 1))
                    pe.transpose(ps[0:T * F, 1, 0:P], s_attr, ident[:]).then_inc(sc["turned", n], 1)
                    pe.wait_ge(sc["turn_copied", n], t + 1)
                    last = pe.matmul(ps[:, 2, 0:D], attr_t[:, 0, :], w_attr[:, 0, :], start=True, stop=True)
                last.then_inc(sc["made", n], 1)
                pe.wait_ge(sc["masked", n], t + 1)
                pe.matmul(ps[:, 4, 0:KA], s_eq, s_msg, start=True, stop=True).then_inc(sc["summed", n], 1)

            with pe.Fori(0, NT) as t:
                tile(t)
            tile(NT)
            pe.sem_inc(sc["back_turned", n], 1)
            with pe.Fori(0, N // BP) as i:
                pe.wait_ge(sc["back_in", n], 16 * (i + 1))
                wait_apart(pe, sc["back_copied", n], i + 1)
                pe.transpose(ps[0:KA, 5, 0:BP], s_back[0:BP, :], ident[0:BP, 0:BP]).then_inc(sc["back_turned", n], 1)

        def scattered_sums(dve, n):
            chain = Chain(dve, sc["chain", n])
            chain(dve.memset(acc[:], 0.0))
            dve.sem_inc(sc["cleared", n], 1)
            dve.wait_ge(sc["consts", n], 6)
            chain(dve.tensor_copy(s_spare, s_spare_i))

            def tile(t, valid):
                dve.wait_ge(sc["ids", n], 64 * (t + 1))
                chain(dve.tensor_copy(s_dstf, s_dst))
                dve.sem_inc(sc["dst_float", n], 1)
                dve.wait_ge(sc["turned", n], t + 1)
                chain(dve.tensor_scalar(s_eq, ps[:, 0, 0:P], s_dstf, None, ALU.is_equal))
                chain(dve.tensor_tensor(s_tmp, s_eq, s_tri, ALU.mult))
                chain(dve.tensor_reduce(s_dup, s_tmp, X, ALU.max))
                chain(dve.tensor_tensor(s_row_f, s_spare, s_dstf, ALU.subtract))
                chain(dve.scalar_tensor_tensor(out=s_row_f, in0=s_row_f, scalar=s_dup, in1=s_dstf, op0=ALU.mult, op1=ALU.add))
                chain(dve.tensor_copy(s_out_i, s_row_f))
                dve.wait_ge(sc["made", n], t + 1)
                if n == 0:
                    chain(dve.tensor_copy(s_typf, s_typ))
                    chain(dve.tensor_scalar(s_mask, iota_f[:, 0:R], s_typf, None, ALU.is_equal))
                    both = ps[:, 2:4, :].rearrange("p a b -> p (a b)").rearrange("p (r m) -> p r m", m=D)
                    chain(dve.tensor_tensor(s_prod, both, s_mask.rearrange("p (r a) -> p r a", a=1).broadcast_to([P, R, D]), ALU.mult))
                    chain(dve.tensor_reduce(s_msg[:, 0:D], s_prod.rearrange("p r m -> p m r"), X, ALU.add))
                else:
                    dve.wait_ge(sc["gathered", n], 32 * (t + 1))
                    chain(dve.tensor_tensor(s_pre, ps[:, 2, 0:D], rows[:, 0, 0, :], ALU.add))
                    for part in (2, 1, 0):
                        chain(dve.tensor_tensor(s_pre, s_pre, s_q[:, part * D:(part + 1) * D], ALU.add))
                    chain(dve.tensor_scalar(s_msg[:, 0:D], s_pre, 0.0, None, ALU.max))
                chain(dve.memset(s_msg[:, D:KA], 1.0))
                dve.tensor_scalar(s_msg, s_msg, valid, None, ALU.mult).then_inc(sc["masked", n], 1)
                dve.wait_ge(sc["summed", n], t + 1)
                dve.tensor_copy(s_comb, ps[:, 4, 0:KA]).then_inc(sc["placed", n], 1)

            links = 12 if n == 0 else 13
            with dve.Fori(0, NT) as t:
                chain.enter(t, links)
                tile(t, ones[:])
                chain.leave(NT)
            tile(NT, s_tail)
            dve.sem_inc(sc["back_copied", n], 1)
            with dve.Fori(0, N // BP) as i:
                dve.wait_ge(sc["back_turned", n], i + 2)
                dve.tensor_copy(acc[0:KA, bass.ds(i * BP, BP)], ps[0:KA, 5, 0:BP]).then_inc(sc["back_copied", n], 1)
            dve.wait_ge(sc["back_copied", n], N // BP + 1)

        @block.sync
        def _(sp):
            def load_edges(v, to, s):
                for part, rows_of in zip(group_rows(v), (to[:, 0, :], to[0:HG - 1, 1, :], to[HG - 1:HG, 1, :])):
                    sp.dma_start(rows_of, part).then_inc(s, 16)

            def load_x(k):
                p, cols, rows_of = piece(k)
                sp.dma_start(by_chunk(xs[0:p, cols, :], k), rows_of(x)).then_inc(x_in[k], 16)

            load_x(0)
            load_edges(dst, dst_i, ids_in[0])
            load_x(1)
            load_x(2)
            load_edges(src, src_i, ids_in[1])
            for k in range(3, NA):
                load_x(k)
            load_edges(edge_type, typ_i, ids_in[2])
            sp.dma_start(base_row[0:1, 0:G - 1, :].rearrange("a g t -> a (g t)"),
                         dst[0:(G - 1) * GE].rearrange("(a t p) -> a t p", a=1, p=P)[:, :, 0], allow_slow_non_contiguous=True).then_inc(base_in, 16)
            sp.dma_start(base_row[0:1, G - 1, :],
                         dst[LAST:E].rearrange("(a t p) -> a t p", a=1, p=P)[:, :, 0], allow_slow_non_contiguous=True).then_inc(base_in, 16)
            for k in range(NA):
                p, cols, rows_of = piece(k)
                sp.wait_ge(h_made_a, k + 1)
                sp.dma_start(rows_of(h_table), by_chunk(h_a[k % 2][0:p, 0:cols.stop - cols.start, :], k)).then_inc(h_stored[k % 2], 16)
            sp.wait_ge(consts_made, 6)
            sp.dma_start(q_table[N:N + P, :], zrows[:]).then_inc(q_stored, 16)
            sp.sem_inc(chunk_stored, 1)

            def store_pq(c, nodes):
                wait_apart(sp, pq_copied, c + 1)
                sp.dma_start(node_rows(p_table, c), p_out[0:nodes.p, 0:nodes.n, :]).then_inc(p_stored, 16)
                wait_apart(sp, q_split, c + 1)
                sp.dma_start(node_rows(q_table[0:N, :], c), q3[0:nodes.p, 0:nodes.n].rearrange("p i s d -> p i (s d)")).then_inc(q_stored, 16)
                wait_apart(sp, p_stored, 16 * (c + 1))
                wait_apart(sp, q_stored, 16 * (c + 2))
                sp.sem_inc(chunk_stored, 1)

            sp.wait_ge(flag_made, 1)
            fits = sp.value_load(flag[0:1, 0:1], min_val=0, max_val=1)
            with sp.If(fits > 0):
                sp.wait_ge(prep_copied, 4)

                def group(it, u):
                    g = it * U + u
                    wait_apart(sp, slots_summed, 2 * (g + 1))
                    sp.dma_start(idx[:, u, :], src_tab[:, bass.ds(g, 1), :]).then_inc(idx0_in[u], 16)

                segments(sp, group, store_pq, at_end=True)
            with sp.Else():
                scattered_loads(sp, 0)
                all_chunks(sp, store_pq)
            store_pq(NC, last_nodes)

            def store_out(c, nodes):
                wait_apart(sp, out_added, c + 2)
                cols = slice(NC * CI, NCOL) if nodes is last_nodes else bass.ds(c * CI, CI)
                sp.dma_start(node_rows(out, c), xs[0:nodes.p, cols, :]).then_inc(out_stored, 16)

            sp.wait_ge(base_in, 32)
            with sp.If(fits > 0):
                sp.wait_ge(starts_made, 1)
                begin = sp.value_load(start_row[0:1, 0:1], min_val=0, max_val=LAST)
                sp.dma_start(attr[:, 0, :], edge_attr[bass.ds(begin, GE), :].rearrange("(p j) f -> p (j f)", j=T)).then_inc(attr_in[0], 16)

                def group(it, u):
                    g = it * U + u
                    begin = sp.value_load(start_row[0:1, bass.ds(g, 1)], min_val=0, max_val=LAST)
                    base = sp.value_load(base_row[0:1, bass.ds(g, 1), 0], min_val=0, max_val=N - 1)
                    after = sp.value_load(start_row[0:1, bass.ds(g + 1, 1)], min_val=0, max_val=LAST)
                    wait_apart(sp, z_made, g + 1)
                    sp.dma_start(idx[:, u, :], src[bass.ds(begin, GE)].rearrange("(p j) -> p j", j=T)).then_inc(idx1_in[u], 16)
                    sp.dma_start(q_win[:, u, :], q_table[bass.ds(base, P), :]).then_inc(q_in[u], 16)
                    wait_apart(sp, group_turned, AHEAD + g - 2)
                    sp.dma_start(attr[:, (u + 1) % U, :],
                                 edge_attr[bass.ds(after, GE), :].rearrange("(p j) f -> p (j f)", j=T)).then_inc(attr_in[(u + 1) % U], 16)

                segments(sp, group, store_out, at_end=True)
            with sp.Else():
                scattered_loads(sp, 1)
                all_chunks(sp, store_out)
            store_out(NC, last_nodes)
            sp.wait_ge(out_stored, 16 * (NC + 1))

        @block.gpsimd
        def _(pool):
            for v in (ident[:], again[:]):
                pool.memset(v, 0.0).then_inc(pool_chain, 1)
            pool.wait_ge(pool_chain, 2)
            pool.affine_select(out=ident[:], in_=ident[:], compare_op=ALU.not_equal, fill=1.0, base=0,
                               pattern=[[-1, P]], channel_multiplier=1).then_inc(consts_made, 1)
            pool.iota(iota_i[:], pattern=[[1, PAR * C0]], base=0, channel_multiplier=0).then_inc(consts_made, 1)
            pool.iota(start_row[:], pattern=[[1, G + 1]], base=0, channel_multiplier=0).then_inc(consts_made, 1)
            pool.memset(attr_t[:], 1.0).then_inc(consts_made, 1)
            pool.memset(zrows[:], 0.0).then_inc(consts_made, 1)
            pool.affine_select(out=again[:], in_=again[:], compare_op=ALU.not_equal, fill=FAR, base=-(HG - 1),
                               pattern=[[0, DUP]], channel_multiplier=1).then_inc(consts_made, 1)
            pool.iota(limit_i[:], pattern=[[HG, 2]], base=-(SEG // 2 * U), channel_multiplier=1).then_inc(consts_made, 1)
            pool.wait_ge(consts_made, 7)
            pool.wait_ge(ids_in[0], 48)
            for a in range(2):
                tiles_of = lambda v: v[:, a, :].rearrange("g (t p) -> g t p", p=P)
                pool.tensor_tensor(tiles_of(off0), tiles_of(dst_i), tiles_of(dst_i)[:, :, 0:1].broadcast_to([HG, T, P]),
                                   ALU.subtract).then_inc(offsets_made, 1)
            pool.wait_ge(offsets_made, 2)
            for k in range(NA):
                p, cols, _ = piece(k)
                n = cols.stop - cols.start
                pool.wait_ge(rstd_made_a, k + 1)
                if k == NA - 1:
                    pool.wait_ge(scaled_a, k)
                v = xc_a[k % 4][0:p, 0:n, :]
                pool.tensor_tensor(v, v, stat_a[0:p, k, 3, 0:n].rearrange("p (i a) -> p i a", a=1).broadcast_to([p, n, D]),
                                   ALU.mult).then_inc(scaled_a, 1)

            pool.wait_ge(flag_made, 1)
            fits = pool.value_load(flag[0:1, 0:1], min_val=0, max_val=1)
            pool.wait_ge(scaled_a, NA)
            for b in range(2):
                pool.wait_ge(h_stored[b], 16 * ((NA + 1 - b) // 2))
            with pool.If(fits > 0):
                with pool.Fori(0, NIT) as it:
                    for u in range(U):
                        wait_apart(pool, idx0_in[u], 16 * (it + 1))
                        for t in range(T):
                            pool.indirect_dma_start(rows[:, u, t, :], None, h_table,
                                                    bass.IndirectOffsetOnAxis(ap=idx[:, u, t:t + 1], axis=0)).then_inc(rows0_in[u], 16)
            with pool.Else():
                scattered_gathers(pool, 0)

            pool.wait_ge(chunk_stored, NC + 2)
            with pool.If(fits > 0):
                with pool.Fori(0, NIT) as it:
                    for u in range(U):
                        wait_apart(pool, idx1_in[u], 16 * (it + 1))
                        for j in range(T):
                            pool.indirect_dma_start(rows[:, u, j, :], None, p_table,
                                                    bass.IndirectOffsetOnAxis(ap=idx[:, u, j:j + 1], axis=0)).then_inc(rows1_in[u], 16)
            with pool.Else():
                scattered_gathers(pool, 1)

        @block.scalar
        def _(act):
            act.sem_inc(relu_made, AHEAD)
            act.wait_ge(blocks_cleared, 1)
            for par in range(PAR):
                act.dma_start(w_pairs[par * D:(par + 1) * D], rel_weight.rearrange("(r a) k m -> a k r m", a=PAR)[par]).then_inc(weights_in, 16)
            act.dma_start(w_all[:], rel_weight.rearrange("r k m -> k r m")).then_inc(weights_in, 16)
            for half in range(2):
                for a in range(2):
                    act.dma_start(w1ab[half * D:(half + 1) * D, half, a * D:(a + 1) * D], w1[a * D:(a + 1) * D, :]).then_inc(weights_in, 16)
            for j in range(T):
                act.dma_start(w_attr[j * F:(j + 1) * F, j, :], w1[2 * D:2 * D + F, :]).then_inc(weights_in, 16)
                act.dma_start(w_attr[T * F:T * F + 1, j, :], b1.rearrange("(a m) -> a m", a=1)).then_inc(weights_in, 16)
            act.dma_start(w2b[0:D, :], w2).then_inc(weights_in, 16)
            act.dma_start(w2b[D:KA, :], b2.rearrange("(a m) -> a m", a=1)).then_inc(weights_in, 16)

            def copy_table(n):
                table, a, half = (src_tab, key0, key1)[n // 4], n // 2 % 2, n % 2
                act.wait_ge(prep_turned, n + 1)
                act.copy(table[:, a * HG:(a + 1) * HG, half * 4:half * 4 + 4].rearrange("p g t -> p t g"),
                         ps[:, n % 4, 0:4 * HG].rearrange("p (t g) -> p t g", g=HG)).then_inc(prep_copied, 1)

            for k in range(NA + 2):
                if k >= 2:
                    p, cols, _ = piece(k - 2)
                    n = cols.stop - cols.start
                    act.wait_ge(scaled_a, k - 1)
                    if k >= 4:
                        act.wait_ge(h_stored[k % 2], 16 * (k // 2 - 1))
                    act.activation(h_a[k % 2][0:p, 0:n, :], xc_a[(k - 2) % 4][0:p, 0:n, :], ACT.Relu).then_inc(h_made_a, 1)
                if k < NA:
                    p, cols, _ = piece(k)
                    n = cols.stop - cols.start
                    act.wait_ge(centered_a, k + 1)
                    act.activation(sq_a[k % 2][0:p, 0:n, :], xc_a[k % 4][0:p, 0:n, :], ACT.Square).then_inc(squared_a, 1)
                if 1 <= k <= NA:
                    p, cols, _ = piece(k - 1)
                    n = cols.stop - cols.start
                    act.wait_ge(var_made_a, k)
                    act.activation(stat_a[0:p, k - 1, 2, 0:n], stat_a[0:p, k - 1, 1, 0:n], ACT.Sqrt, bias=eps[0:p, :], scale=1.0 / D).then_inc(std_made_a, 1)
                if k == 3:
                    act.wait_ge(ids_in[1], 48)
                    act.copy(src_f, src_i).then_inc(src_float, 1)
                if k == 5:
                    for n in range(4):
                        copy_table(n)
            for n in range(4, 12):
                copy_table(n)

            def chunk_pq(c, nodes, ready=None):
                p, n = nodes.p, nodes.n
                if ready is not None:
                    ready(c)
                act.wait_ge(turned, c + 1)
                act.copy(stage[0:D, 0:p * n], acc[0:D, (slice(LN0, N) if nodes is last_nodes else bass.ds(c * CN, CN))]).then_inc(staged, 1)
                act.wait_ge(centered, c + 1)
                act.activation(sq[0:p, 0:n], xc[0:p, 0:n], ACT.Square).then_inc(squared, 1)
                act.wait_ge(var_made, c + 1)
                act.activation(stat[0:p, 2, 0:n], stat[0:p, 1, 0:n], ACT.Sqrt, bias=eps[0:p, :], scale=1.0 / D).then_inc(std_made, 1)
                act.wait_ge(h_turned, c + 2)
                act.wait_ge(pq_made, c + 1)
                act.copy(h_t[:, 0:n // 2, 0:p], nodes.ht).then_inc(ht_copied, 1)
                act.wait_ge(chunk_stored, c + 1)
                act.wait_ge(pq_made, c + 2)
                act.copy(p_out[0:p, 0:n, :], nodes.pq[:, :, 0, :])
                act.copy(q3[0:p, 0:n, 0, :], nodes.pq[:, :, 1, :]).then_inc(pq_copied, 1)
                act.wait_ge(rest_made, c + 2)
                act.copy(q3[0:p, 0:n, 1, :], q_rest[0:p, 0:n, :]).then_inc(part2_made, 1)

            act.wait_ge(flag_made, 1)
            fits = act.value_load(flag[0:1, 0:1], min_val=0, max_val=1)
            with act.If(fits > 0):
                def group(it, u):
                    g = it * U + u
                    act.wait_ge(typed, g + 3)
                    for half in range(2):
                        act.wait_ge(slots_summed, 2 * AHEAD + 2 * g + half + 1)
                        t = slice(half * T // 2, (half + 1) * T // 2)
                        act.copy(slots[:, u % 2, t, :], slot_ps[:, u % 2, t, :]).then_inc(slots_copied, 1)

                def ready(c):
                    act.wait_ge(window_added, T * (AHEAD + ((c + 1) * SEG + SEG // 2) * U))

                segments(act, group, lambda c, nodes: chunk_pq(c, nodes, ready))
            with act.Else():
                scattered_copies(act, 0)
                act.wait_ge(layer0_summed, 1)
                all_chunks(act, chunk_pq)
            act.wait_ge(layer0_summed, 1)
            chunk_pq(NC, last_nodes)

            def chunk_out(c, nodes, ready=None):
                if ready is not None:
                    ready(c)
                act.wait_ge(out_made, c + 1)
                act.copy(stage[0:KA, 0:nodes.p * nodes.n],
                         acc[0:KA, (slice(LN0, N) if nodes is last_nodes else bass.ds(c * CN, CN))]).then_inc(out_staged, 1)

            with act.If(fits > 0):
                def copy_turned(g, b):
                    act.wait_ge(group_turned, AHEAD + g + 1)
                    act.wait_ge(pre_made, g + 3)
                    act.copy(attr_t[0:T * F, b, :], attrt_ps).then_inc(turn_copied, 1)
                    for half in range(2):
                        cols = slice(half * 512, (half + 1) * 512)
                        act.copy(onehot_t[:, b, cols], oht_ps[:, cols]).then_inc(turn_copied, 1)

                def group(it, u):
                    g = it * U + u
                    act.wait_ge(pre_added, g + AHEAD + 1)
                    act.wait_ge(z_made, g + 3)
                    act.activation(relus[:, u % 2, :, 0:D], presum[:, u % 2, 0:T * D].rearrange("p (t d) -> p t d", d=D),
                                   ACT.Relu).then_inc(relu_made, 1)
                    copy_turned(g + 1, (u + 1) % 2)

                def ready(c):
                    act.wait_ge(z_added, AHEAD + ((c + 1) * SEG + SEG // 2) * U)

                copy_turned(0, 0)
                segments(act, group, lambda c, nodes: chunk_out(c, nodes, ready))
            with act.Else():
                scattered_copies(act, 1)
                act.wait_ge(layer1_summed, 1)
                all_chunks(act, chunk_out)
            act.wait_ge(layer1_summed, 1)
            chunk_out(NC, last_nodes)

        @block.vector
        def _(dve):
            chain = Chain(dve, dve_chain)
            wide = lambda v, p, n: v.rearrange("p (i a) -> p i a", a=1).broadcast_to([p, n, D])
            dve.memset(ones[:], 1.0)
            dve.memset(eps[:], 1e-5)
            dve.memset(w1ab[:], 0.0)
            chain(dve.memset(w_attr[:], 0.0))
            dve.sem_inc(blocks_cleared, 1)
            for key in (key0, key1):
                dve.memset(key[:, G, :], FAR)
            dve.memset(relus[:, :, :, D:KA], 1.0)
            dve.sem_inc(rest_made, 1)
            dve.sem_inc(out_added, 1)

            def check_edges():
                e = extremes[0:HG]
                heads = dst_i.rearrange("g a (t p) -> g a t p", p=P)[:, :, :, 0]
                tops = dst_i[:, :, 0]
                tmp, tmp2 = stat_a[0:HG, NA - 1, 0, :].rearrange("g (a t) -> g a t", t=T), stat_a[0:HG, NA - 1, 1, 0:2]
                dve.wait_ge(consts_made, 7)
                chain(dve.tensor_single_scalar(limit_i[:], limit_i[:], (SEG * U).bit_length() - 1, ALU.arith_shift_right))
                chain(dve.tensor_scalar(limit[:], limit_i[:], float(CN), None, ALU.mult))
                chain(dve.tensor_tensor(tmp, heads, tops.rearrange("g (a t) -> g a t", t=1).broadcast_to([HG, 2, T]), ALU.subtract))
                chain(dve.tensor_tensor(tmp2, tops, limit[:], ALU.subtract))
                dve.tensor_reduce(e[:, 2:3], tmp, mybir.AxisListType.XY, ALU.max)
                dve.tensor_reduce(e[:, 3:4], tmp, mybir.AxisListType.XY, ALU.min)
                dve.tensor_reduce(e[:, 4:5], tmp2, X, ALU.min)
                dve.wait_ge(offsets_made, 2)
                dve.tensor_reduce(e[:, 0:1], off0, mybir.AxisListType.XY, ALU.max)
                chain(dve.tensor_reduce(e[:, 1:2], off0, mybir.AxisListType.XY, ALU.min))
                bad = e[:, 5:6]
                chain(dve.tensor_scalar(bad, e[:, 0:1], float(W0), None, ALU.is_ge))
                for col, op, bound in ((1, ALU.is_lt, 0.0), (2, ALU.is_gt, float(W1N - W0)), (3, ALU.is_lt, 0.0), (4, ALU.is_lt, 0.0)):
                    chain(dve.scalar_tensor_tensor(out=bad, in0=e[:, col:col + 1], scalar=bound, in1=bad, op0=op, op1=ALU.add))
                dve.sem_inc(bad_made, 1)

            for k in range(NA + 1):
                if k < NA:
                    p, cols, _ = piece(k)
                    n = cols.stop - cols.start
                    dve.wait_ge(x_in[k], 16)
                    xv = xs[0:p, cols, :]
                    chain(dve.tensor_reduce(stat_a[0:p, k, 0, 0:n], xv, X, ALU.add))
                    if k >= 4:
                        dve.wait_ge(h_made_a, k - 3)
                    dve.scalar_tensor_tensor(out=xc_a[k % 4][0:p, 0:n, :], in0=wide(stat_a[0:p, k, 0, 0:n], p, n), scalar=-1.0 / D, in1=xv,
                                             op0=ALU.mult, op1=ALU.add).then_inc(centered_a, 1)
                if k == 1:
                    check_edges()
                if k == 3:
                    dve.wait_ge(bad_summed, 1)
                    dve.tensor_scalar(flag[:], ps[0:1, 4, 0:1], 0.5, None, ALU.is_lt).then_inc(flag_made, 1)
                if k >= 1:
                    p, cols, _ = piece(k - 1)
                    n = cols.stop - cols.start
                    dve.wait_ge(squared_a, k)
                    dve.tensor_reduce(stat_a[0:p, k - 1, 1, 0:n], sq_a[(k - 1) % 2][0:p, 0:n, :], X, ALU.add).then_inc(var_made_a, 1)
                    dve.wait_ge(std_made_a, k)
                    dve.reciprocal(stat_a[0:p, k - 1, 3, 0:n], stat_a[0:p, k - 1, 2, 0:n]).then_inc(rstd_made_a, 1)

            dve.wait_ge(ids_in[2], 48)
            chain(dve.tensor_single_scalar(par_i, typ_i, 1, ALU.bitwise_and))
            chain(dve.scalar_tensor_tensor(out=typ_f, in0=par_i, scalar=float((C0 - W0 // PAR) // (W0 // PAR)), in1=typ_i, op0=ALU.mult, op1=ALU.add))
            chain(dve.scalar_tensor_tensor(out=key0_g, in0=typ_f, scalar=float(W0 // PAR), in1=off0, op0=ALU.mult, op1=ALU.add))
            chain(dve.tensor_tensor(key1_g, dst_i, dst_i[:, :, 0:1].broadcast_to([HG, 2, GE]), ALU.subtract))
            lo = (HG - 1) // 32 * 32
            for key in (key0_g, key1_g):
                v = key[lo:HG, 1, 0:DUP]
                dve.tensor_tensor(v, v, again[lo:HG, :], ALU.add).then_inc(keys_made, 1)
            dve.tensor_copy(iota_f[:], iota_i[:])
            chain(dve.tensor_scalar(start_row[:], start_row[:], float(GE), float(LAST), ALU.mult, ALU.min))
            dve.sem_inc(starts_made, 1)

            def chunk_pq(c, nodes):
                p, n = nodes.p, nodes.n
                xv = xs[0:p, (slice(NC * CI, NCOL) if nodes is last_nodes else bass.ds(c * CI, CI)), :]
                s1, var, std, rstd = (stat[0:p, m, 0:n] for m in range(4))
                dve.wait_ge(turned, c + 2)
                dve.tensor_tensor(xv, xv, nodes.x, ALU.add).then_inc(x_added, 1)
                wait_apart(dve, x_added, c + 1)
                dve.tensor_reduce(s1, xv, X, ALU.add).then_inc(x_added_sum, 1)
                dve.wait_ge(x_added_sum, c + 1)
                dve.scalar_tensor_tensor(out=xc[0:p, 0:n], in0=wide(s1, p, n), scalar=-1.0 / D, in1=xv, op0=ALU.mult, op1=ALU.add).then_inc(centered, 1)
                dve.wait_ge(squared, c + 1)
                dve.tensor_reduce(var, sq[0:p, 0:n], X, ALU.add).then_inc(var_made, 1)
                dve.wait_ge(std_made, c + 1)
                dve.reciprocal(rstd, std).then_inc(rstd_made, 1)
                dve.wait_ge(rstd_made, c + 1)
                dve.wait_ge(h_turned, c + 1)
                dve.scalar_tensor_tensor(out=h[0:p, 0:n], in0=xc[0:p, 0:n], scalar=0.0, in1=wide(rstd, p, n), op0=ALU.max, op1=ALU.mult).then_inc(h_made, 1)
                dve.wait_ge(pq_copied, c + 1)
                dve.tensor_tensor(q_rest[0:p, 0:n], nodes.pq[:, :, 1, :], q3[0:p, 0:n, 0, :], ALU.subtract).then_inc(rest_made, 1)
                dve.wait_ge(part2_made, c + 1)
                dve.tensor_tensor(q3[0:p, 0:n, 2, :], q_rest[0:p, 0:n], q3[0:p, 0:n, 1, :], ALU.subtract).then_inc(q_split, 1)

            dve.wait_ge(flag_made, 1)
            fits = dve.value_load(flag[0:1, 0:1], min_val=0, max_val=1)
            dve.wait_ge(h_made_a, NA)
            with dve.If(fits > 0):
                dve.sem_inc(window_added, AHEAD * T)
                dve.wait_ge(prep_copied, 8)

                def make_onehot0(g, b):
                    dve.wait_ge(slots_summed, 2 * AHEAD + 2 * g - 2)
                    dve.tensor_tensor(onehot[:, b], key0[:, bass.ds(g, 1), :].rearrange("p a (t c) -> p (a t) c", c=1).broadcast_to([P, T, PAR * C0]),
                                      iota_f[:].rearrange("p (a c) -> p a c", a=1).broadcast_to([P, T, PAR * C0]), ALU.is_equal).then_inc(onehot0, 1)

                make_onehot0(0, 0)
                dve.wait_ge(prep_turned, 12)
                chain(dve.memset(acc[:], 0.0))
                dve.wait_ge(base_in, 32)

                def group(it, u):
                    g = it * U + u
                    make_onehot0(g + 1, (u + 1) % 2)
                    _, bases = nc.values_load_multi_w_load_instructions(
                        base_row[0:1, bass.ds(g, 1), :].rearrange("a g t -> a (g t)"), engines=[ENG.DVE], min_val=0, max_val=N - 1,
                        skip_runtime_bounds_check_because="dst holds nodes' numbers")
                    dve.wait_ge(typed, AHEAD + g + 1)
                    for t in range(T):
                        window = acc[0:D, bass.ds(bases[t], W0)]
                        dve.wait_ge(window_added, AHEAD * T + g * T + t)
                        dve.tensor_tensor(window, window, node_ps[:, u % 2, t * W0:(t + 1) * W0], ALU.add).then_inc(window_added, 1)

                segments(dve, group, chunk_pq)
                dve.wait_ge(window_added, (AHEAD + G) * T)
                dve.sem_inc(layer0_summed, 1)
            with dve.Else():
                dve.wait_ge(prep_turned, 12)
                scattered_sums(dve, 0)
                dve.sem_inc(layer0_summed, 1)
                all_chunks(dve, chunk_pq)
            chunk_pq(NC, last_nodes)

            def chunk_out(c, nodes):
                xv = xs[0:nodes.p, (slice(NC * CI, NCOL) if nodes is last_nodes else bass.ds(c * CI, CI)), :]
                dve.wait_ge(out_made, c + 2)
                dve.tensor_tensor(xv, xv, nodes.out, ALU.add).then_inc(out_added, 1)

            dve.wait_ge(staged, NC + 1)
            with dve.If(fits > 0):
                dve.sem_inc(pre_added, AHEAD)
                oh1 = onehot[:, :, :, 0:P]

                def make_onehot1(g, b):
                    dve.wait_ge(z_made, AHEAD + g - 1)
                    dve.tensor_tensor(oh1[:, b], key1[:, bass.ds(g, 1), :].rearrange("p a (t c) -> p (a t) c", c=1).broadcast_to([P, T, P]),
                                      iota_f[:, 0:P].rearrange("p (a c) -> p a c", a=1).broadcast_to([P, T, P]), ALU.is_equal).then_inc(onehot1, 1)

                dve.wait_ge(prep_copied, 12)
                make_onehot1(0, 0)
                dve.memset(acc[:], 0.0).then_inc(z_added, AHEAD)

                def group(it, u):
                    g, b = it * U + u, u % 2
                    make_onehot1(g + 1, (u + 1) % 2)
                    base = dve.value_load(base_row[0:1, bass.ds(g, 1), 0], min_val=0, max_val=N - 1)
                    dve.wait_ge(pre_made, AHEAD + g + 1)
                    dve.wait_ge(rows1_in[u], 16 * T * (it + 1))
                    dve.wait_ge(relu_made, g + AHEAD - 1)
                    dve.tensor_tensor(presum[:, b, 0:T * D], pre_ps[:, b, :], rows[:, u].rearrange("p t d -> p (t d)"), ALU.add).then_inc(pre_added, 1)
                    dve.wait_ge(z_made, AHEAD + g + 1)
                    window = acc[0:KA, bass.ds(base, W1N)]
                    dve.wait_ge(z_added, AHEAD + g)
                    dve.tensor_tensor(window, window, z_ps[:, b, 0:W1N], ALU.add).then_inc(z_added, 1)

                segments(dve, group, chunk_out)
                dve.wait_ge(z_added, AHEAD + G)
                dve.sem_inc(layer1_summed, 1)
            with dve.Else():
                scattered_sums(dve, 1)
                dve.sem_inc(layer1_summed, 1)
                all_chunks(dve, chunk_out)
            chunk_out(NC, last_nodes)

        @block.tensor
        def _(pe):
            for s, n in ((slots_summed, 2 * AHEAD), (typed, AHEAD), (pre_made, AHEAD), (z_made, AHEAD), (group_turned, AHEAD),
                         (turned, 1), (h_turned, 1), (pq_made, 1), (out_made, 1)):
                pe.sem_inc(s, n)
            pe.wait_ge(consts_made, 1)
            for n in range(12):
                v = (src_f, key0_g, key1_g)[n // 4][:, n // 2 % 2, :]
                v = v.rearrange("g (p j) -> g j p", j=T) if n >= 8 else v.rearrange("g (t p) -> g t p", p=P)
                if n == 0:
                    pe.wait_ge(bad_made, 1)
                    pe.matmul(ps[0:1, 4, 0:1], extremes[0:HG, 5:6], ones[0:HG, :], start=True, stop=True).then_inc(bad_summed, 1)
                    pe.wait_ge(src_float, 1)
                elif n % 4 == 0:
                    pe.wait_ge(keys_made, n // 4)
                if n >= 4:
                    pe.wait_ge(prep_copied, n - 3)
                for t in range(4):
                    last = pe.transpose(ps[:, n % 4, t * HG:(t + 1) * HG], v[:, n % 2 * 4 + t, :], ident[0:HG, 0:HG])
                last.then_inc(prep_turned, 1)

            def chunk_pq(c, nodes):
                p, n = nodes.p, nodes.n
                pe.wait_ge(staged, c + 1)
                wait_apart(pe, rest_made, c + 1)
                for i in range(n):
                    last = pe.transpose(nodes.x[:, i, :], nodes.stage[0:D, i, :], ident[0:D, 0:D])
                last.then_inc(turned, 1)
                wait_apart(pe, h_made, c + 1)
                for i in range(n // 2):
                    last = pe.transpose(nodes.ht[:, i, :], h[0:p, 2 * i:2 * i + 2, :].rearrange("p i d -> p (i d)"), ident[0:p, 0:p])
                last.then_inc(h_turned, 1)
                wait_apart(pe, ht_copied, c + 1)
                for i in range(n // 2):
                    last = pe.matmul(nodes.pq[:, 2 * i:2 * i + 2].rearrange("p i a d -> p (i a d)"), h_t[:, i, 0:p],
                                     w1ab[:].rearrange("k a n -> k (a n)"), start=True, stop=True)
                last.then_inc(pq_made, 1)

            pe.wait_ge(flag_made, 1)
            fits = pe.value_load(flag[0:1, 0:1], min_val=0, max_val=1)
            pe.wait_ge(prep_copied, 12)
            pe.wait_ge(weights_in, 16 * (PAR + 1 + 4 + 2 * T + 2))
            with pe.If(fits > 0):
                def group(it, u):
                    g, b = it * U + u, u % 2
                    pe.wait_ge(onehot0, g + 1)
                    pe.wait_ge(rows0_in[u], 16 * T * (it + 1))
                    for t in range(T):
                        for par in range(PAR):
                            last = pe.matmul(slot_ps[par * D:(par + 1) * D, b, t, :], rows[:, u, t, :],
                                             onehot[:, b, t, par * C0:(par + 1) * C0], start=True, stop=True)
                        if t % 4 == 3:
                            last.then_inc(slots_summed, 1)
                    pe.wait_ge(slots_copied, 2 * (g + 1))
                    pe.wait_ge(window_added, T * (g + AHEAD - 1))
                    for r in range(RP):
                        last = pe.matmul(node_ps[:, b, 0:T * W0], w_pairs[:, r, :], slots[:, b, :, r * W0:(r + 1) * W0],
                                         start=(r == 0), stop=(r == RP - 1))
                    last.then_inc(typed, 1)

                segments(pe, group, chunk_pq)
            with pe.Else():
                scattered_products(pe, 0)
                all_chunks(pe, chunk_pq)
            chunk_pq(NC, last_nodes)

            def chunk_out(c, nodes):
                pe.wait_ge(out_staged, c + 1)
                pe.wait_ge(out_added, c + 1)
                for i in range(nodes.n):
                    last = pe.matmul(nodes.out[:, i, :], nodes.stage[0:KA, i, :], w2b[:], start=True, stop=True)
                last.then_inc(out_made, 1)

            pe.wait_ge(rest_made, NC + 2)
            with pe.If(fits > 0):
                def turn_group(g, b, at):
                    pe.wait_ge(attr_in[at[0]], 16 * at[1])
                    wait_apart(pe, onehot1, g + 1)
                    pe.transpose(attrt_ps, attr[:, at[0], :], ident[:])
                    for j in range(T):
                        last = pe.transpose(oht_ps[:, j * P:(j + 1) * P], onehot[:, b, j, 0:P], ident[:])
                    last.then_inc(group_turned, 1)

                def group(it, u):
                    g, b = it * U + u, u % 2
                    pe.wait_ge(turn_copied, 3 * (g + 1))
                    pe.wait_ge(q_in[u], 16 * (it + 1))
                    pe.wait_ge(pre_added, g + AHEAD - 1)
                    pe.matmul(pre_ps[:, b, :], attr_t[:, b, :], w_attr[:].rearrange("k j d -> k (j d)"), start=True, stop=False)
                    for j in range(T):
                        for part in range(3):
                            last = pe.matmul(pre_ps[:, b, j * D:(j + 1) * D], onehot_t[:, b, j * P:(j + 1) * P],
                                             q_win[:, u, part * D:(part + 1) * D], start=False, stop=(j == T - 1 and part == 2))
                    last.then_inc(pre_made, 1)
                    turn_group(g + 1, (u + 1) % 2, ((u + 1) % U, it + 1 + (u + 1) // U))
                    pe.wait_ge(relu_made, AHEAD + g + 1)
                    pe.wait_ge(z_added, g + AHEAD - 1)
                    for j in range(T):
                        last = pe.matmul(z_ps[:, b, 0:W1N], relus[:, b, j, :], onehot[:, b, j, 0:P], start=(j == 0), stop=(j == T - 1))
                    last.then_inc(z_made, 1)

                turn_group(0, 0, (0, 1))
                segments(pe, group, chunk_out)
                pe.wait_ge(turn_copied, 3 * (G + 1))
            with pe.Else():
                scattered_products(pe, 1)
                all_chunks(pe, chunk_out)
            chunk_out(NC, last_nodes)


_INS = ['x', 'src', 'dst', 'edge_attr_8', 'edge_type_16', 'L0_gnn_weight', 'L1_gnn_W1', 'L1_gnn_b1', 'L1_gnn_W2', 'L1_gnn_b2']


def kernel(**inputs):
    import numpy as _np
    import concourse.bacc as _bacc
    from concourse import mybir as _mybir
    from concourse.bass_utils import run_bass_kernel_spmd as _run

    nc = _bacc.Bacc("TRN2", target_bir_lowering=False, num_devices=1)
    arrays, args = {}, []
    for name in _INS:
        a = _np.ascontiguousarray(inputs[name])
        arrays[f"in_{name}_dram"] = a
        args.append(nc.dram_tensor(f"in_{name}_dram", a.shape, _mybir.dt.from_np(a.dtype), kind="ExternalInput").ap())
    shape = inputs["x"].shape
    args.append(nc.dram_tensor("out_0_dram", shape, _mybir.dt.float32, kind="ExternalOutput").ap())
    gnn_kernel(nc, *args)
    r = _run(nc, [arrays], core_ids=[0])
    return r.results[0]["out_0_dram"]
```

```python
import concourse.bass as bass
import concourse.mybir as mybir
from concourse.alu_op_type import AluOpType as ALU
from contextlib import ExitStack


def gnn_kernel(nc, x, src, dst, edge_attr, edge_type, rel_weight, w1, b1, w2, b2, out):
    fp32, bf16, i32 = mybir.dt.float32, mybir.dt.bfloat16, mybir.dt.int32
    ACT = mybir.ActivationFunctionType
    X = mybir.AxisListType.X
    ENG = mybir.EngineType

    P = 128
    N, D = x.shape
    E, F = edge_attr.shape
    R = rel_weight.shape[0]
    PAR = 2
    RP = R // PAR
    T = 8
    GE = T * P
    G = -(-E // GE)
    LAST = E - GE
    DUP = GE * (G - 1) - LAST
    HG = G // 2
    U = 8
    V = 4
    NIT = G // U
    W0 = 16
    W1N = P
    C0 = RP * W0
    NSEG = 13
    SEG = NIT // NSEG
    CP, CI = 120, 8
    CN = CP * CI
    NC = NSEG - 1
    LP, LI = 98, 10
    LN0 = NC * CN
    NCOL = NC * CI + LI
    AC = 2
    NA = NC // AC + 1
    KA = D + 1
    ACCN = N + P
    BP = 125
    NT = E // P
    AHEAD = U
    EG = 6
    NWL = 2 + 1 + 4 + T + 3
    PG = 2
    NK = NA + EG // PG
    FAR = float(1 << 20)
    assert PG * T == AC * CI and U - EG == PG and EG < U and G % U == 0 and G % 2 == 0 and LN0 + LP * LI == N and 0 < DUP and NIT == NSEG * SEG and SEG % 2 == 0

    ctx = ExitStack()
    with ctx:
        def sb(name, shape, dt):
            return ctx.enter_context(nc.sbuf_tensor(name, shape, dt))

        def sem(name):
            return ctx.enter_context(nc.semaphore(name))

        def dram(name, shape, dt):
            return nc.dram_tensor(name, shape, dt, kind="Internal").ap()

        h_table = dram("h_table", (N, D), fp32)
        p_table = dram("p_table", (N, D), fp32)
        q_table = dram("q_table", (N + P, 3 * D), bf16)
        SROWS = P * (-(-(N + P) // P))
        sums0 = dram("sums0", (SROWS, KA), fp32)
        sums1 = dram("sums1", (SROWS, KA), fp32)

        acc = sb("acc", [P, ACCN], fp32)
        xs = sb("xs", [P, NCOL, D], fp32)
        src_tab = sb("src_tab", [P, G, T], i32)
        key0 = sb("key0", [P, G + 1, T], fp32)
        key1 = sb("key1", [P, G + 1, T], fp32)
        base_row = sb("base_row", [1, G, T], i32)
        start_row = sb("start_row", [1, G + 1], i32)
        idx = sb("idx", [P, U, T], i32)
        rows = sb("rows", [P, U, T, D], fp32)
        onehot = sb("onehot", [P, 2, T, PAR * C0], fp32)
        slots = sb("slots", [P, 2, T, C0], fp32)
        relus = sb("relus", [P, 2, T, KA], fp32)
        onehot_t = sb("onehot_t", [P, 2, T * P], bf16)
        attr = sb("attr", [P, V, T * F], fp32)
        attr_t = sb("attr_t", [T * F + 1, 2, P], fp32)
        q_win = sb("q_win", [P, V, 3 * D], bf16)
        stage = sb("stage", [P, LP * LI], fp32)
        xc = sb("xc", [P, LI, D], fp32)
        sq = sb("sq", [P, LI, D], fp32)
        h = sb("h", [P, LI, D], fp32)
        h_t = sb("h_t", [P, LI // 2, CP], fp32)
        p_out = sb("p_out", [P, LI, D], fp32)
        q_rest = sb("q_rest", [P, LI, D], fp32)
        q3 = sb("q3", [P, LI, 3, D], bf16)
        stat = sb("stat", [P, 4, LI], fp32)
        stat_a = sb("stat_a", [P, NK, 4, AC * CI], fp32)
        first_src = sb("first_src", [EG * T, P], i32)
        first_f = sb("first_f", [EG * T, P], fp32)
        ident = sb("ident", [P, P], fp32)
        iota_i = sb("iota_i", [P, PAR * C0], i32)
        iota_f = sb("iota_f", [P, PAR * C0], fp32)
        zero = sb("zero", [P, 1], fp32)
        ones = sb("ones", [P, 1], fp32)
        eps = sb("eps", [P, 1], fp32)
        zrows = sb("zrows", [P, 3 * D], bf16)
        w_pairs = sb("w_pairs", [P, RP, D], fp32)
        w_all = sb("w_all", [D, R, D], fp32)
        w_attr = sb("w_attr", [T * F + 1, T, D], fp32)
        again = sb("again", [P, DUP], fp32)
        limit_i = sb("limit_i", [HG, 2], i32)
        limit = sb("limit", [HG, 2], fp32)
        w1ab = sb("w1ab", [P, 2, 2 * D], fp32)
        w2b = sb("w2b", [KA, D], fp32)
        extremes = sb("extremes", [P, 6], fp32)
        flag = sb("flag", [1, 1], i32)

        def edge_list(n, dt):
            v = acc[0:HG, n * 2 * GE:(n + 1) * 2 * GE]
            return (v.bitcast(i32) if dt == i32 else v).rearrange("g (a e) -> g a e", a=2)
        dst_i, src_i, typ_i = edge_list(0, i32), edge_list(1, i32), edge_list(2, i32)
        off0, par_i, typ_f = edge_list(3, i32), edge_list(4, i32), edge_list(5, fp32)
        src_f, key0_g, key1_g = edge_list(1, fp32), edge_list(4, fp32), edge_list(2, fp32)

        flat_oh = onehot[:].rearrange("p a b c -> p (a b c)")
        PW = AC * CI
        ring = lambda v, n: v[:, n * PW * D:(n + 1) * PW * D].rearrange("p (i d) -> p i d", d=D)
        xc_a = [ring(flat_oh, n) for n in range(4)] + [rows[:, EG:U].rearrange("p u t d -> p (u t) d")]
        XR = len(xc_a)
        sq_a = [ring(slots[:].rearrange("p b t c -> p (b t c)"), n) for n in range(2)]
        sq_first = relus[:, :, :, 0:D].rearrange("p b t d -> p (b t) d")
        presum = slots[:].rearrange("p b t c -> p b (t c)")

        s_row = slots[:].rearrange("p b t c -> p (b t c)")
        s_prod = s_row[:, 0:R * D].rearrange("p (r m) -> p r m", m=D)
        s_eq, s_tri, s_tmp = flat_oh[:, 0:P], flat_oh[:, P:2 * P], flat_oh[:, 2 * P:3 * P]
        s_gt = flat_oh[:, 3 * P:4 * P]
        s_msg = flat_oh[:, 4 * P:4 * P + KA]
        s_comb = flat_oh[:, 5 * P:5 * P + KA]
        s_dstf, s_typf = flat_oh[:, 6 * P:6 * P + 1], flat_oh[:, 6 * P + 1:6 * P + 2]
        s_dup, s_row_f = flat_oh[:, 6 * P + 2:6 * P + 3], flat_oh[:, 6 * P + 3:6 * P + 4]
        s_spare, s_tail = flat_oh[:, 6 * P + 4:6 * P + 5], flat_oh[:, 6 * P + 5:6 * P + 6]
        s_mask = flat_oh[:, 6 * P + 8:6 * P + 8 + R]
        s_attr = flat_oh[:, 7 * P:7 * P + T * F]
        s_back = flat_oh[:, 9 * P:9 * P + KA]
        s_pre = flat_oh[:, 10 * P:10 * P + D]
        s_spare_i = idx[:, 0, 4:5]
        s_src, s_dst, s_typ, s_out_i = idx[:, 0, 0:1], idx[:, 0, 1:2], idx[:, 0, 2:3], idx[:, 0, 3:4]
        s_q = q_win[:, 0, :]

        ps = ctx.enter_context(nc.psum_tensor("ps", [P, 8, 512], fp32))
        ps_all = ps[:].rearrange("p a b -> p (a b)")
        slot_ps = ps_all[:, 0:4 * 512].rearrange("p (b t c) -> p b t c", b=2, t=T)
        node_ps = ps_all[0:D, 4 * 512:6 * 512].rearrange("k (b n) -> k b n", b=2)
        oht_ps = ps_all[:, 0:2 * 512]
        attrt_ps = ps[0:T * F, 2, 0:P]
        pre_ps = ps_all[:, 3 * 512:5 * 512].rearrange("p (b c) -> p b c", b=2)
        z_ps = ps_all[0:KA, 5 * 512:7 * 512].rearrange("k (b n) -> k b n", b=2)

        class Nodes:

            def __init__(self, p, n, x_bank, ht_bank, p_bank, q_bank, out_bank):
                self.p, self.n = p, n
                at = lambda bank, w: ps_all[:, bank * 512:bank * 512 + w]
                self.x = at(x_bank, n * D)[0:p].rearrange("p (i d) -> p i d", d=D)
                self.ht = at(ht_bank, n // 2 * P).rearrange("k (i p) -> k i p", p=P)[:, :, 0:p]
                self.pq = [at(bank, n * D)[0:p].rearrange("p (i d) -> p i d", d=D) for bank in (p_bank, q_bank)]
                self.out = at(out_bank, n * D)[0:p].rearrange("p (i d) -> p i d", d=D)
                self.stage = stage[:, 0:p * n].rearrange("k (p i) -> k i p", i=n)

        chunk_nodes, last_nodes = Nodes(CP, CI, 6, 7, 6, 7, 7), Nodes(LP, LI, 0, 2, 4, 6, 0)

        ids_in = [sem(f"ids_in_{k}") for k in range(3)]
        x_in = [sem(f"x_in_{k}") for k in range(NA)]
        weights_in = sem("weights_in")
        base_in = sem("base_in")
        consts_made = sem("consts_made")
        pool_chain = sem("pool_chain")
        dve_chain = sem("dve_chain")
        starts_made = sem("starts_made")
        src_float = sem("src_float")
        offsets_made = sem("offsets_made")
        keys_made = sem("keys_made")
        bad_made = sem("bad_made")
        bad_summed = sem("bad_summed")
        flag_made = sem("flag_made")
        prep_turned = sem("prep_turned")
        prep_copied = sem("prep_copied")
        centered_a = sem("centered_a")
        squared_a = sem("squared_a")
        var_made_a = sem("var_made_a")
        std_made_a = sem("std_made_a")
        rstd_made_a = sem("rstd_made_a")
        first_in = sem("first_in")
        first_float = sem("first_float")
        first_turned = sem("first_turned")
        first_idx = sem("first_idx")
        zero_made = sem("zero_made")
        acc_cleared = sem("acc_cleared")
        h_made_a = sem("h_made_a")
        h_stored = [sem(f"h_stored_{b}") for b in range(XR)]
        blocks_cleared = sem("blocks_cleared")
        idx_in = [sem(f"idx_in_{u}") for u in range(U)]
        rows_in = [sem(f"rows_in_{u}") for u in range(U)]
        onehot0 = sem("onehot0")
        slots_summed = sem("slots_summed")
        slots_copied = sem("slots_copied")
        typed = sem("typed")
        window_added = sem("window_added")
        layer0_summed = sem("layer0_summed")
        staged = sem("staged")
        turned = sem("turned")
        x_added = sem("x_added")
        x_added_sum = sem("x_added_sum")
        rstd_made = sem("rstd_made")
        centered = sem("centered")
        squared = sem("squared")
        var_made = sem("var_made")
        std_made = sem("std_made")
        h_made = sem("h_made")
        h_turned = sem("h_turned")
        ht_copied = sem("ht_copied")
        p_made = sem("p_made")
        pq_made = sem("pq_made")
        p_copied = sem("p_copied")
        pq_copied = sem("pq_copied")
        rest_made = sem("rest_made")
        part2_made = sem("part2_made")
        q_split = sem("q_split")
        p_stored = sem("p_stored")
        q_stored = sem("q_stored")
        chunk_stored = sem("chunk_stored")
        q_in = [sem(f"q_in_{u}") for u in range(V)]
        attr_in = [sem(f"attr_in_{u}") for u in range(V)]
        onehot1 = sem("onehot1")
        group_turned = sem("group_turned")
        turn_copied = sem("turn_copied")
        pre_made = sem("pre_made")
        pre_added = sem("pre_added")
        relu_made = sem("relu_made")
        z_made = sem("z_made")
        z_added = sem("z_added")
        layer1_summed = sem("layer1_summed")
        out_staged = sem("out_staged")
        out_made = sem("out_made")
        out_added = sem("out_added")
        out_stored = sem("out_stored")
        sc = {(k, n): sem(f"scattered{n}_{k}") for n in range(2)
              for k in ("consts", "cleared", "zeroed", "ids", "gathered", "dst_float", "turned", "turn_copied", "made",
                        "masked", "summed", "placed", "added", "back_in", "back_turned", "back_copied", "chain")}

        waited = {e: sem(f"waited_{n}") for e, n in ((ENG.SP, "sync"), (ENG.Pool, "gpsimd"), (ENG.DVE, "vector"), (ENG.PE, "tensor"))}

        block = ctx.enter_context(nc.Block())

        class Chain:

            def __init__(self, eng, s, wait=None):
                self.eng, self.s, self.at, self.n = eng, s, 0, 0
                self.wait = wait or (lambda eng, s, value: eng.wait_ge(s, value))

            def __call__(self, ins):
                self.n += 1
                ins.then_inc(self.s, 1)
                self.wait(self.eng, self.s, self.at + self.n)

            def enter(self, i, k):
                self.before = self.at + self.n
                self.at, self.n, self.k = self.before + i * k, 0, k

            def leave(self, turns):
                assert self.n == self.k, (self.n, self.k)
                self.at, self.n = self.before + turns * self.k, 0

        def group_rows(v):
            return (v[0:HG * GE].rearrange("(g e) -> g e", e=GE),
                    v[HG * GE:(G - 1) * GE].rearrange("(g e) -> g e", e=GE),
                    v[LAST:E].rearrange("(g e) -> g e", e=GE))

        def wait_apart(eng, s, value):
            eng.wait_ge(s, value)
            eng.sem_inc(waited[eng.engine], 1)

        def node_rows(v, c):
            if isinstance(c, int) and c == NC:
                return v[LN0:N, :].rearrange("(p i) d -> p i d", i=LI)
            return v[0:LN0, :].rearrange("(c p i) d -> c p i d", p=CP, i=CI)[bass.ds(c, 1)].rearrange("c p i d -> p (c i) d")

        def piece(k):
            if k == NA - 1:
                return LP, slice(NC * CI, NCOL), lambda v: node_rows(v, NC)
            rows_of = lambda v: v[k * AC * CN:(k + 1) * AC * CN, :].rearrange("(c p i) d -> p c i d", p=CP, i=CI)
            return CP, slice(k * AC * CI, (k + 1) * AC * CI), rows_of

        def normed(k):
            if k >= NA:
                v = rows[:, (k - NA) * PG:(k - NA + 1) * PG].rearrange("p u t d -> p (u t) d")
                return P, PG * T, v, v, sq_first
            p, cols, _ = piece(k)
            n = cols.stop - cols.start
            return p, n, xs[0:p, cols, :], xc_a[k % XR][0:p, 0:n, :], sq_a[k % 2][0:p, 0:n, :]

        def by_chunk(v, k):
            return v if k == NA - 1 else v.rearrange("p (c i) d -> p c i d", i=CI)

        def segments(eng, group_body, chunk, at_end=False, begin=0):
            def iterations(first, n):
                with eng.Fori(first, first + n) as it:
                    for u in range(U):
                        group_body(it, u)
            iterations(begin, SEG - begin)
            with eng.Fori(1, NSEG) as s:
                with eng.Fori(0, SEG // 2) as i:
                    for u in range(U):
                        group_body(s * SEG + i, u)
                if not at_end:
                    chunk(s - 1, chunk_nodes)
                with eng.Fori(SEG // 2, SEG) as i:
                    for u in range(U):
                        group_body(s * SEG + i, u)
                if at_end:
                    chunk(s - 1, chunk_nodes)

        def all_chunks(eng, chunk):
            with eng.Fori(0, NC) as c:
                chunk(c, chunk_nodes)

        def scattered_loads(sp, n):
            sums = (sums0, sums1)[n]
            sp.wait_ge(sc["cleared", n], 1)
            sp.dma_start(sums.rearrange("(p r) k -> p (r k)", p=P), acc[:, 0:SROWS // P * KA]).then_inc(sc["zeroed", n], 16)

            def tile(t, first):
                for v, to in ((src, s_src), (dst, s_dst), (edge_type, s_typ)):
                    sp.dma_start(to, v[bass.ds(first, P)].rearrange("(p a) -> p a", a=1)).then_inc(sc["ids", n], 16)
                sp.dma_start(s_attr[:, 0:F], edge_attr[bass.ds(first, P), :]).then_inc(sc["ids", n], 16)

            sp.wait_ge(sc["zeroed", n], 16)
            sp.wait_ge(sc["consts", n], 6)
            tile(0, 0)
            with sp.Fori(1, NT) as t:
                wait_apart(sp, sc["added", n], 16 * t)
                tile(t, t * P)
            sp.wait_ge(sc["added", n], 16 * NT)
            tile(NT, E - P)
            sp.wait_ge(sc["added", n], 16 * (NT + 1))
            with sp.Fori(0, N // BP) as i:
                wait_apart(sp, sc["back_turned", n], i + 1)
                sp.dma_start(s_back[0:BP, :], sums[bass.ds(i * BP, BP), :]).then_inc(sc["back_in", n], 16)

        def scattered_gathers(pool, n):
            sums, gathers = (sums0, sums1)[n], (1, 2)[n]
            pool.iota(s_spare_i, pattern=[[0, 1]], base=N, channel_multiplier=1).then_inc(sc["consts", n], 1)
            pool.memset(s_tri, 1.0).then_inc(sc["consts", n], 1)
            pool.memset(s_tail, 1.0).then_inc(sc["consts", n], 1)
            pool.memset(s_attr, 0.0).then_inc(sc["consts", n], 1)
            pool.wait_ge(sc["consts", n], 4)
            pool.affine_select(out=s_tri, in_=s_tri, compare_op=ALU.is_gt, fill=0.0, base=0,
                               pattern=[[-1, P]], channel_multiplier=1).then_inc(sc["consts", n], 1)
            pool.affine_select(out=s_tail, in_=s_tail, compare_op=ALU.is_ge, fill=0.0, base=-(P - (E - NT * P)),
                               pattern=[[0, 1]], channel_multiplier=1).then_inc(sc["consts", n], 1)

            def tile(t):
                wait_apart(pool, sc["ids", n], 64 * (t + 1))
                pool.indirect_dma_start(rows[:, 0, 0, :], None, (h_table, p_table)[n],
                                        bass.IndirectOffsetOnAxis(ap=s_src, axis=0)).then_inc(sc["gathered", n], 16)
                if n == 1:
                    pool.indirect_dma_start(s_q, None, q_table,
                                            bass.IndirectOffsetOnAxis(ap=s_dst, axis=0)).then_inc(sc["gathered", n], 16)
                wait_apart(pool, sc["placed", n], t + 1)
                pool.indirect_dma_start(sums, bass.IndirectOffsetOnAxis(ap=s_out_i, axis=0), s_comb, None,
                                        compute_op=ALU.add).then_inc(sc["added", n], 16)

            with pool.Fori(0, NT) as t:
                tile(t)
            tile(NT)

        def scattered_copies(act, n):
            def tile(t):
                act.wait_ge(sc["turned", n], t + 1)
                if n == 0:
                    act.copy(s_gt[0:D, :], ps[0:D, 1, 0:P]).then_inc(sc["turn_copied", n], 1)
                else:
                    act.copy(attr_t[0:T * F, 0, :], ps[0:T * F, 1, 0:P]).then_inc(sc["turn_copied", n], 1)

            with act.Fori(0, NT) as t:
                tile(t)
            tile(NT)

        def scattered_products(pe, n):
            def tile(t):
                pe.wait_ge(sc["dst_float", n], t + 1)
                pe.matmul(ps[:, 0, 0:P], s_dstf.broadcast_to([P, P]), ident[:], start=True, stop=True)
                if n == 0:
                    wait_apart(pe, sc["gathered", n], 16 * (t + 1))
                    pe.transpose(ps[0:D, 1, 0:P], rows[:, 0, 0, :], ident[:]).then_inc(sc["turned", n], 1)
                    pe.wait_ge(sc["turn_copied", n], t + 1)
                    for half in range(2):
                        r = slice(half * R // 2, (half + 1) * R // 2)
                        last = pe.matmul(ps[:, 2 + half, :], s_gt[0:D, :], w_all[:, r, :].rearrange("k r m -> k (r m)"), start=True, stop=True)
                else:
                    wait_apart(pe, sc["ids", n], 64 * (t + 1))
                    pe.transpose(ps[0:T * F, 1, 0:P], s_attr, ident[:]).then_inc(sc["turned", n], 1)
                    pe.wait_ge(sc["turn_copied", n], t + 1)
                    last = pe.matmul(ps[:, 2, 0:D], attr_t[:, 0, :], w_attr[:, 0, :], start=True, stop=True)
                last.then_inc(sc["made", n], 1)
                pe.wait_ge(sc["masked", n], t + 1)
                pe.matmul(ps[:, 4, 0:KA], s_eq, s_msg, start=True, stop=True).then_inc(sc["summed", n], 1)

            with pe.Fori(0, NT) as t:
                tile(t)
            tile(NT)
            pe.sem_inc(sc["back_turned", n], 1)
            with pe.Fori(0, N // BP) as i:
                pe.wait_ge(sc["back_in", n], 16 * (i + 1))
                wait_apart(pe, sc["back_copied", n], i + 1)
                pe.transpose(ps[0:KA, 5, 0:BP], s_back[0:BP, :], ident[0:BP, 0:BP]).then_inc(sc["back_turned", n], 1)

        def scattered_sums(dve, n):
            chain = Chain(dve, sc["chain", n])
            chain(dve.memset(acc[:], 0.0))
            dve.sem_inc(sc["cleared", n], 1)
            dve.wait_ge(sc["consts", n], 6)
            chain(dve.tensor_copy(s_spare, s_spare_i))

            def tile(t, valid):
                dve.wait_ge(sc["ids", n], 64 * (t + 1))
                chain(dve.tensor_copy(s_dstf, s_dst))
                dve.sem_inc(sc["dst_float", n], 1)
                dve.wait_ge(sc["turned", n], t + 1)
                chain(dve.tensor_scalar(s_eq, ps[:, 0, 0:P], s_dstf, None, ALU.is_equal))
                chain(dve.tensor_tensor(s_tmp, s_eq, s_tri, ALU.mult))
                chain(dve.tensor_reduce(s_dup, s_tmp, X, ALU.max))
                chain(dve.tensor_tensor(s_row_f, s_spare, s_dstf, ALU.subtract))
                chain(dve.scalar_tensor_tensor(out=s_row_f, in0=s_row_f, scalar=s_dup, in1=s_dstf, op0=ALU.mult, op1=ALU.add))
                chain(dve.tensor_copy(s_out_i, s_row_f))
                dve.wait_ge(sc["made", n], t + 1)
                if n == 0:
                    chain(dve.tensor_copy(s_typf, s_typ))
                    chain(dve.tensor_scalar(s_mask, iota_f[:, 0:R], s_typf, None, ALU.is_equal))
                    both = ps[:, 2:4, :].rearrange("p a b -> p (a b)").rearrange("p (r m) -> p r m", m=D)
                    chain(dve.tensor_tensor(s_prod, both, s_mask.rearrange("p (r a) -> p r a", a=1).broadcast_to([P, R, D]), ALU.mult))
                    chain(dve.tensor_reduce(s_msg[:, 0:D], s_prod.rearrange("p r m -> p m r"), X, ALU.add))
                else:
                    dve.wait_ge(sc["gathered", n], 32 * (t + 1))
                    chain(dve.tensor_tensor(s_pre, ps[:, 2, 0:D], rows[:, 0, 0, :], ALU.add))
                    for part in (2, 1, 0):
                        chain(dve.tensor_tensor(s_pre, s_pre, s_q[:, part * D:(part + 1) * D], ALU.add))
                    chain(dve.tensor_scalar(s_msg[:, 0:D], s_pre, 0.0, None, ALU.max))
                chain(dve.memset(s_msg[:, D:KA], 1.0))
                dve.tensor_scalar(s_msg, s_msg, valid, None, ALU.mult).then_inc(sc["masked", n], 1)
                dve.wait_ge(sc["summed", n], t + 1)
                dve.tensor_copy(s_comb, ps[:, 4, 0:KA]).then_inc(sc["placed", n], 1)

            links = 12 if n == 0 else 13
            with dve.Fori(0, NT) as t:
                chain.enter(t, links)
                tile(t, ones[:])
                chain.leave(NT)
            tile(NT, s_tail)
            dve.sem_inc(sc["back_copied", n], 1)
            with dve.Fori(0, N // BP) as i:
                dve.wait_ge(sc["back_turned", n], i + 2)
                dve.tensor_copy(acc[0:KA, bass.ds(i * BP, BP)], ps[0:KA, 5, 0:BP]).then_inc(sc["back_copied", n], 1)
            dve.wait_ge(sc["back_copied", n], N // BP + 1)

        @block.sync
        def _(sp):
            def load_edges(v, to, s):
                for part, rows_of in zip(group_rows(v), (to[:, 0, :], to[0:HG - 1, 1, :], to[HG - 1:HG, 1, :])):
                    sp.dma_start(rows_of, part).then_inc(s, 16)

            def load_x(k):
                p, cols, rows_of = piece(k)
                sp.dma_start(by_chunk(xs[0:p, cols, :], k), rows_of(x)).then_inc(x_in[k], 16)

            sp.dma_start(first_src[:], src[0:EG * GE].rearrange("(c p) -> c p", p=P)).then_inc(first_in, 16)
            load_x(0)
            load_edges(dst, dst_i, ids_in[0])
            load_x(1)
            load_x(2)
            load_edges(src, src_i, ids_in[1])
            for k in range(3, NA):
                load_x(k)
            load_edges(edge_type, typ_i, ids_in[2])
            sp.dma_start(base_row[0:1, 0:G - 1, :].rearrange("a g t -> a (g t)"),
                         dst[0:(G - 1) * GE].rearrange("(a t p) -> a t p", a=1, p=P)[:, :, 0], allow_slow_non_contiguous=True).then_inc(base_in, 16)
            sp.dma_start(base_row[0:1, G - 1, :],
                         dst[LAST:E].rearrange("(a t p) -> a t p", a=1, p=P)[:, :, 0], allow_slow_non_contiguous=True).then_inc(base_in, 16)
            for k in range(NA):
                p, cols, rows_of = piece(k)
                sp.wait_ge(h_made_a, k + 1)
                sp.dma_start(rows_of(h_table), by_chunk(xc_a[k % XR][0:p, 0:cols.stop - cols.start, :], k)).then_inc(h_stored[k % XR], 16)
            sp.wait_ge(consts_made, 6)
            sp.dma_start(q_table[N:N + P, :], zrows[:]).then_inc(q_stored, 16)
            sp.sem_inc(chunk_stored, 1)

            def store_pq(c, nodes):
                wait_apart(sp, p_copied, c + 1)
                sp.dma_start(node_rows(p_table, c), p_out[0:nodes.p, 0:nodes.n, :]).then_inc(p_stored, 16)
                wait_apart(sp, q_split, c + 1)
                sp.dma_start(node_rows(q_table[0:N, :], c), q3[0:nodes.p, 0:nodes.n].rearrange("p i s d -> p i (s d)")).then_inc(q_stored, 16)
                wait_apart(sp, p_stored, 16 * (c + 1))
                wait_apart(sp, q_stored, 16 * (c + 2))
                sp.sem_inc(chunk_stored, 1)

            sp.wait_ge(flag_made, 1)
            fits = sp.value_load(flag[0:1, 0:1], min_val=0, max_val=1)
            with sp.If(fits > 0):
                sp.wait_ge(prep_copied, 4)
                for u in range(EG, U):
                    sp.dma_start(idx[:, u, :], src_tab[:, u, :]).then_inc(idx_in[u], 16)

                def group(it, u):
                    g = it * U + u
                    wait_apart(sp, slots_summed, 2 * (g + 1))
                    sp.dma_start(idx[:, u, :], src_tab[:, bass.ds(g, 1), :]).then_inc(idx_in[u], 16)

                segments(sp, group, store_pq, at_end=True, begin=1)
                sp.wait_ge(slots_summed, 2 * (AHEAD + G))
                for u in range(U):
                    sp.dma_start(idx[:, u, :], src[u * GE:(u + 1) * GE].rearrange("(p j) -> p j", j=T)).then_inc(idx_in[u], 16)
            with sp.Else():
                for u in range(EG):
                    sp.wait_ge(rows_in[u], 16 * T)
                scattered_loads(sp, 0)
                all_chunks(sp, store_pq)
            store_pq(NC, last_nodes)

            def store_out(c, nodes):
                wait_apart(sp, out_added, c + 2)
                cols = slice(NC * CI, NCOL) if nodes is last_nodes else bass.ds(c * CI, CI)
                sp.dma_start(node_rows(out, c), xs[0:nodes.p, cols, :]).then_inc(out_stored, 16)

            sp.wait_ge(base_in, 32)
            with sp.If(fits > 0):
                sp.wait_ge(starts_made, 1)
                begin = sp.value_load(start_row[0:1, 0:1], min_val=0, max_val=LAST)
                sp.dma_start(attr[:, 0, :], edge_attr[bass.ds(begin, GE), :].rearrange("(p j) f -> p (j f)", j=T)).then_inc(attr_in[0], 16)

                def group(it, u, first=False):
                    g = it * U + u
                    base = sp.value_load(base_row[0:1, bass.ds(g, 1), 0], min_val=0, max_val=N - 1)
                    after = sp.value_load(start_row[0:1, bass.ds(g + 1, 1)], min_val=0, max_val=LAST)
                    if not first:
                        begin = sp.value_load(start_row[0:1, bass.ds(g, 1)], min_val=0, max_val=LAST)
                        wait_apart(sp, z_made, g + 1)
                        sp.dma_start(idx[:, u, :], src[bass.ds(begin, GE)].rearrange("(p j) -> p j", j=T)).then_inc(idx_in[u], 16)
                    if not first or u >= V:
                        wait_apart(sp, z_made, AHEAD + g - V + 1)
                    sp.dma_start(q_win[:, u % V, :], q_table[bass.ds(base, P), :]).then_inc(q_in[u % V], 16)
                    wait_apart(sp, group_turned, AHEAD + g + 2 - V)
                    sp.dma_start(attr[:, (u + 1) % V, :],
                                 edge_attr[bass.ds(after, GE), :].rearrange("(p j) f -> p (j f)", j=T)).then_inc(attr_in[(u + 1) % V], 16)

                for u in range(U):
                    group(0, u, first=True)
                segments(sp, group, store_out, at_end=True, begin=1)
            with sp.Else():
                scattered_loads(sp, 1)
                all_chunks(sp, store_out)
            store_out(NC, last_nodes)
            sp.wait_ge(out_stored, 16 * (NC + 1))

        @block.gpsimd
        def _(pool):
            for v in (ident[:], again[:]):
                pool.memset(v, 0.0).then_inc(pool_chain, 1)
            pool.wait_ge(pool_chain, 2)
            pool.affine_select(out=ident[:], in_=ident[:], compare_op=ALU.not_equal, fill=1.0, base=0,
                               pattern=[[-1, P]], channel_multiplier=1).then_inc(consts_made, 1)
            pool.iota(iota_i[:], pattern=[[1, PAR * C0]], base=0, channel_multiplier=0).then_inc(consts_made, 1)
            pool.iota(start_row[:], pattern=[[1, G + 1]], base=0, channel_multiplier=0).then_inc(consts_made, 1)
            pool.memset(attr_t[:], 1.0).then_inc(consts_made, 1)
            pool.memset(zrows[:], 0.0).then_inc(consts_made, 1)
            pool.affine_select(out=again[:], in_=again[:], compare_op=ALU.not_equal, fill=FAR, base=-(HG - 1),
                               pattern=[[0, DUP]], channel_multiplier=1).then_inc(consts_made, 1)
            pool.iota(limit_i[:], pattern=[[HG, 2]], base=-(SEG // 2 * U), channel_multiplier=1).then_inc(consts_made, 1)
            pool.wait_ge(consts_made, 7)
            def gather(table, u, t, s):
                pool.indirect_dma_start(rows[:, u, t, :], None, table,
                                        bass.IndirectOffsetOnAxis(ap=idx[:, u, t:t + 1], axis=0)).then_inc(s, 16)

            pool.wait_ge(first_idx, 1)
            for u in range(EG):
                if u == 1:
                    pool.wait_ge(ids_in[0], 48)
                    for a in range(2):
                        tiles_of = lambda v: v[:, a, :].rearrange("g (t p) -> g t p", p=P)
                        pool.tensor_tensor(tiles_of(off0), tiles_of(dst_i), tiles_of(dst_i)[:, :, 0:1].broadcast_to([HG, T, P]),
                                           ALU.subtract).then_inc(offsets_made, 1)
                for t in range(T):
                    gather(x, u, t, rows_in[u])

            pool.wait_ge(flag_made, 1)
            fits = pool.value_load(flag[0:1, 0:1], min_val=0, max_val=1)
            for b in range(XR):
                pool.wait_ge(h_stored[b], 16 * len(range(b, NA, XR)))
            with pool.If(fits > 0):
                for u in range(EG, U):
                    pool.wait_ge(idx_in[u], 16)
                    for t in range(T):
                        gather(h_table, u, t, rows_in[u])
                with pool.Fori(1, NIT) as it:
                    for u in range(U):
                        wait_apart(pool, idx_in[u], 16 * (it + 1) if u >= EG else 16 * it)
                        for t in range(T):
                            gather(h_table, u, t, rows_in[u])
            with pool.Else():
                pool.wait_ge(h_made_a, NK)
                scattered_gathers(pool, 0)

            pool.wait_ge(p_stored, 16 * (NC + 1))
            with pool.If(fits > 0):
                with pool.Fori(0, NIT) as it:
                    for u in range(U):
                        wait_apart(pool, idx_in[u], 16 * (it + 1 + (NIT if u >= EG else NIT - 1)))
                        for j in range(T):
                            gather(p_table, u, j, rows_in[u])
            with pool.Else():
                pool.wait_ge(chunk_stored, NC + 2)
                scattered_gathers(pool, 1)

        @block.scalar
        def _(act):
            act.sem_inc(relu_made, AHEAD)
            act.wait_ge(blocks_cleared, 1)
            loads = [(w_pairs[par * D:(par + 1) * D], rel_weight.rearrange("(r a) k m -> a k r m", a=PAR)[par]) for par in range(PAR)]
            loads += [(w_all[:], rel_weight.rearrange("r k m -> k r m"))]
            loads += [(w1ab[half * D:(half + 1) * D, half, a * D:(a + 1) * D], w1[a * D:(a + 1) * D, :])
                      for half in range(2) for a in range(2)]
            loads += [(w_attr[j * F:(j + 1) * F, j, :], w1[2 * D:2 * D + F, :]) for j in range(T)]
            loads += [(w_attr[T * F:T * F + 1, :, :], b1.rearrange("(a b m) -> a b m", a=1, b=1).broadcast_to([1, T, D])),
                      (w2b[0:D, :], w2), (w2b[D:KA, :], b2.rearrange("(a m) -> a m", a=1))]
            assert len(loads) == NWL

            def load_weights(k):
                for to, v in loads[k * NWL // (NA - 1):(k + 1) * NWL // (NA - 1)]:
                    act.dma_start(to, v).then_inc(weights_in, 16)

            def copy_table(n):
                table, a, half = (src_tab, key0, key1)[n // 4], n // 2 % 2, n % 2
                act.wait_ge(prep_turned, n + 1)
                act.copy(table[:, a * HG:(a + 1) * HG, half * 4:half * 4 + 4].rearrange("p g t -> p t g"),
                         ps[:, n % 4, 0:4 * HG].rearrange("p (t g) -> p t g", g=HG)).then_inc(prep_copied, 1)

            def norm(k, first, end):
                if k < end:
                    p, n, _, xcv, sqv = normed(k)
                    act.wait_ge(centered_a, k + 1)
                    if k > NA:
                        act.wait_ge(var_made_a, k)
                    act.activation(sqv, xcv, ACT.Square).then_inc(squared_a, 1)
                if k > first:
                    p, n = normed(k - 1)[0:2]
                    act.wait_ge(var_made_a, k)
                    act.activation(stat_a[0:p, k - 1, 2, 0:n], stat_a[0:p, k - 1, 1, 0:n], ACT.Sqrt, bias=eps[0:p, :], scale=1.0 / D).then_inc(std_made_a, 1)

            for k in range(NA + 1):
                norm(k, 0, NA)
                if 1 <= k < NA:
                    load_weights(k - 1)
                if k == 3:
                    act.wait_ge(ids_in[1], 48)
                    act.copy(src_f, src_i).then_inc(src_float, 1)
                if k == 5:
                    for n in range(4):
                        copy_table(n)

            def clear(n):
                act.copy(acc[:, n * 2 * GE:(n + 1) * 2 * GE], zero[:].broadcast_to([P, 2 * GE])).then_inc(acc_cleared, 1)

            act.wait_ge(zero_made, 1)
            clear(1)
            act.wait_ge(keys_made, 1)
            clear(3)
            clear(5)
            for n in range(4, 8):
                copy_table(n)
            for k in range(NA, NK + 1):
                norm(k, NA, NK)
                if k < NA + 2:
                    copy_table(8 + 2 * (k - NA))
                    copy_table(9 + 2 * (k - NA))
            clear(0)

            def chunk_pq(c, nodes, ready=None):
                p, n = nodes.p, nodes.n
                if ready is not None:
                    ready(c)
                act.wait_ge(turned, c + 1)
                act.copy(stage[0:D, 0:p * n], acc[0:D, (slice(LN0, N) if nodes is last_nodes else bass.ds(c * CN, CN))]).then_inc(staged, 1)
                act.wait_ge(centered, c + 1)
                act.activation(sq[0:p, 0:n], xc[0:p, 0:n], ACT.Square).then_inc(squared, 1)
                act.wait_ge(var_made, c + 1)
                act.activation(stat[0:p, 2, 0:n], stat[0:p, 1, 0:n], ACT.Sqrt, bias=eps[0:p, :], scale=1.0 / D).then_inc(std_made, 1)
                act.wait_ge(h_turned, c + 2)
                act.wait_ge(pq_made, c + 1)
                act.copy(h_t[:, 0:n // 2, 0:p], nodes.ht).then_inc(ht_copied, 1)
                act.wait_ge(chunk_stored, c + 1)
                act.wait_ge(p_made, c + 1)
                act.copy(p_out[0:p, 0:n, :], nodes.pq[0]).then_inc(p_copied, 1)
                act.wait_ge(pq_made, c + 2)
                act.copy(q3[0:p, 0:n, 0, :], nodes.pq[1]).then_inc(pq_copied, 1)
                act.wait_ge(rest_made, c + 2)
                act.copy(q3[0:p, 0:n, 1, :], q_rest[0:p, 0:n, :]).then_inc(part2_made, 1)

            act.wait_ge(flag_made, 1)
            fits = act.value_load(flag[0:1, 0:1], min_val=0, max_val=1)
            with act.If(fits > 0):
                def group(it, u):
                    g = it * U + u
                    act.wait_ge(typed, AHEAD + g - 1)
                    for half in range(2):
                        act.wait_ge(slots_summed, 2 * AHEAD + 2 * g + half + 1)
                        t = slice(half * T // 2, (half + 1) * T // 2)
                        act.copy(slots[:, u % 2, t, :], slot_ps[:, u % 2, t, :]).then_inc(slots_copied, 1)

                def ready(c):
                    act.wait_ge(window_added, T * (AHEAD + ((c + 1) * SEG + SEG // 2) * U))

                segments(act, group, lambda c, nodes: chunk_pq(c, nodes, ready))
            with act.Else():
                scattered_copies(act, 0)
                act.wait_ge(layer0_summed, 1)
                all_chunks(act, chunk_pq)
            act.wait_ge(layer0_summed, 1)
            chunk_pq(NC, last_nodes)

            def chunk_out(c, nodes, ready=None):
                if ready is not None:
                    ready(c)
                act.wait_ge(out_made, c + 1)
                act.copy(stage[0:KA, 0:nodes.p * nodes.n],
                         acc[0:KA, (slice(LN0, N) if nodes is last_nodes else bass.ds(c * CN, CN))]).then_inc(out_staged, 1)

            with act.If(fits > 0):
                def copy_turned(g, b):
                    act.wait_ge(group_turned, AHEAD + g + 1)
                    act.wait_ge(pre_made, AHEAD + g - 1)
                    act.copy(attr_t[0:T * F, b, :], attrt_ps).then_inc(turn_copied, 1)
                    for half in range(2):
                        cols = slice(half * 512, (half + 1) * 512)
                        act.copy(onehot_t[:, b, cols], oht_ps[:, cols]).then_inc(turn_copied, 1)

                def group(it, u):
                    g = it * U + u
                    act.wait_ge(pre_added, g + AHEAD + 1)
                    act.wait_ge(z_made, AHEAD + g - 1)
                    act.activation(relus[:, u % 2, :, 0:D], presum[:, u % 2, 0:T * D].rearrange("p (t d) -> p t d", d=D),
                                   ACT.Relu).then_inc(relu_made, 1)
                    copy_turned(g + 1, (u + 1) % 2)

                def ready(c):
                    act.wait_ge(z_added, AHEAD + ((c + 1) * SEG + SEG // 2) * U)

                copy_turned(0, 0)
                segments(act, group, lambda c, nodes: chunk_out(c, nodes, ready))
            with act.Else():
                scattered_copies(act, 1)
                act.wait_ge(layer1_summed, 1)
                all_chunks(act, chunk_out)
            act.wait_ge(layer1_summed, 1)
            chunk_out(NC, last_nodes)

        @block.vector
        def _(dve):
            chain = Chain(dve, dve_chain)
            wide = lambda v, p, n: v.rearrange("p (i a) -> p i a", a=1).broadcast_to([p, n, D])
            dve.memset(ones[:], 1.0)
            dve.memset(zero[:], 0.0).then_inc(zero_made, 1)
            dve.memset(eps[:], 1e-5)
            dve.memset(w1ab[:], 0.0)
            chain(dve.memset(w_attr[:], 0.0))
            dve.sem_inc(blocks_cleared, 1)
            for key in (key0, key1):
                dve.memset(key[:, G, :], FAR)
            dve.memset(relus[:, :, :, D:KA], 1.0)
            dve.sem_inc(rest_made, 1)
            dve.sem_inc(out_added, 1)

            dve.wait_ge(first_in, 16)
            dve.tensor_copy(first_f[:], first_src[:]).then_inc(first_float, 1)
            dve.wait_ge(first_turned, 1)
            dve.tensor_copy(idx[:, 0:EG, :].rearrange("p u t -> p (u t)"), ps[:, 5, 0:EG * T]).then_inc(first_idx, 1)

            def check_edges():
                e = extremes[0:HG]
                heads = dst_i.rearrange("g a (t p) -> g a t p", p=P)[:, :, :, 0]
                tops = dst_i[:, :, 0]
                tmp, tmp2 = stat_a[0:HG, NK - 1, 0, :].rearrange("g (a t) -> g a t", t=T), stat_a[0:HG, NK - 1, 1, 0:2]
                dve.wait_ge(consts_made, 7)
                chain(dve.tensor_single_scalar(limit_i[:], limit_i[:], (SEG * U).bit_length() - 1, ALU.arith_shift_right))
                chain(dve.tensor_scalar(limit[:], limit_i[:], float(CN), None, ALU.mult))
                chain(dve.tensor_tensor(tmp, heads, tops.rearrange("g (a t) -> g a t", t=1).broadcast_to([HG, 2, T]), ALU.subtract))
                chain(dve.tensor_tensor(tmp2, tops, limit[:], ALU.subtract))
                dve.tensor_reduce(e[:, 2:3], tmp, mybir.AxisListType.XY, ALU.max)
                dve.tensor_reduce(e[:, 3:4], tmp, mybir.AxisListType.XY, ALU.min)
                dve.tensor_reduce(e[:, 4:5], tmp2, X, ALU.min)
                dve.wait_ge(offsets_made, 2)
                dve.tensor_reduce(e[:, 0:1], off0, mybir.AxisListType.XY, ALU.max)
                chain(dve.tensor_reduce(e[:, 1:2], off0, mybir.AxisListType.XY, ALU.min))
                bad = e[:, 5:6]
                chain(dve.tensor_scalar(bad, e[:, 0:1], float(W0), None, ALU.is_ge))
                for col, op, bound in ((1, ALU.is_lt, 0.0), (2, ALU.is_gt, float(W1N - W0)), (3, ALU.is_lt, 0.0), (4, ALU.is_lt, 0.0)):
                    chain(dve.scalar_tensor_tensor(out=bad, in0=e[:, col:col + 1], scalar=bound, in1=bad, op0=op, op1=ALU.add))
                dve.sem_inc(bad_made, 1)

            def norm(k, first, end):
                if k < end:
                    p, n, xv, xcv, _ = normed(k)
                    if k < NA:
                        dve.wait_ge(x_in[k], 16)
                    else:
                        for u in range((k - NA) * PG, (k - NA + 1) * PG):
                            dve.wait_ge(rows_in[u], 16 * T)
                    chain(dve.tensor_reduce(stat_a[0:p, k, 0, 0:n], xv, X, ALU.add))
                    if XR <= k < NA:
                        dve.wait_ge(h_stored[k % XR], 16 * (k // XR))
                    dve.scalar_tensor_tensor(out=xcv, in0=wide(stat_a[0:p, k, 0, 0:n], p, n), scalar=-1.0 / D, in1=xv,
                                             op0=ALU.mult, op1=ALU.add).then_inc(centered_a, 1)
                if first < k <= end:
                    p, n, _, _, sqv = normed(k - 1)
                    dve.wait_ge(squared_a, k)
                    dve.tensor_reduce(stat_a[0:p, k - 1, 1, 0:n], sqv, X, ALU.add).then_inc(var_made_a, 1)
                if k > first + 1:
                    p, n, _, xcv, _ = normed(k - 2)
                    dve.wait_ge(std_made_a, k - 1)
                    dve.reciprocal(stat_a[0:p, k - 2, 3, 0:n], stat_a[0:p, k - 2, 2, 0:n]).then_inc(rstd_made_a, 1)
                    dve.wait_ge(rstd_made_a, k - 1)
                    dve.scalar_tensor_tensor(out=xcv, in0=xcv, scalar=0.0, in1=wide(stat_a[0:p, k - 2, 3, 0:n], p, n),
                                             op0=ALU.max, op1=ALU.mult).then_inc(h_made_a, 1)

            for k in range(NA + 2):
                norm(k, 0, NA)
            check_edges()

            dve.wait_ge(ids_in[2], 48)
            chain(dve.tensor_single_scalar(par_i, typ_i, 1, ALU.bitwise_and))
            dve.wait_ge(bad_summed, 1)
            dve.tensor_scalar(flag[:], ps[0:1, 4, 0:1], 0.5, None, ALU.is_lt).then_inc(flag_made, 1)
            chain(dve.scalar_tensor_tensor(out=typ_f, in0=par_i, scalar=float((C0 - W0 // PAR) // (W0 // PAR)), in1=typ_i, op0=ALU.mult, op1=ALU.add))
            chain(dve.scalar_tensor_tensor(out=key0_g, in0=typ_f, scalar=float(W0 // PAR), in1=off0, op0=ALU.mult, op1=ALU.add))
            lo = (HG - 1) // 32 * 32

            def again_far(key):
                v = key[lo:HG, 1, 0:DUP]
                dve.tensor_tensor(v, v, again[lo:HG, :], ALU.add).then_inc(keys_made, 1)

            again_far(key0_g)
            dve.tensor_copy(iota_f[:], iota_i[:])
            chain(dve.tensor_tensor(key1_g, dst_i, dst_i[:, :, 0:1].broadcast_to([HG, 2, GE]), ALU.subtract))
            again_far(key1_g)

            def make_onehot0(g, b):
                dve.wait_ge(slots_summed, 2 * AHEAD + 2 * g - 2)
                dve.tensor_tensor(onehot[:, b], key0[:, bass.ds(g, 1), :].rearrange("p a (t c) -> p (a t) c", c=1).broadcast_to([P, T, PAR * C0]),
                                  iota_f[:].rearrange("p (a c) -> p a c", a=1).broadcast_to([P, T, PAR * C0]), ALU.is_equal).then_inc(onehot0, 1)

            for k in range(NA, NK + 2):
                norm(k, NA, NK)
                if k == NA:
                    chain(dve.tensor_scalar(start_row[:], start_row[:], float(GE), float(LAST), ALU.mult, ALU.min))
                    dve.sem_inc(starts_made, 1)
                    for b in range(XR - 1):
                        dve.wait_ge(h_stored[b], 16 * len(range(b, NA, XR)))
                    dve.wait_ge(prep_copied, 8)
                if k in (NA + 1, NA + 2):
                    make_onehot0(k - NA - 1, (k - NA - 1) % 2)

            def chunk_pq(c, nodes):
                p, n = nodes.p, nodes.n
                xv = xs[0:p, (slice(NC * CI, NCOL) if nodes is last_nodes else bass.ds(c * CI, CI)), :]
                s1, var, std, rstd = (stat[0:p, m, 0:n] for m in range(4))
                dve.wait_ge(turned, c + 2)
                dve.tensor_tensor(xv, xv, nodes.x, ALU.add).then_inc(x_added, 1)
                wait_apart(dve, x_added, c + 1)
                dve.tensor_reduce(s1, xv, X, ALU.add).then_inc(x_added_sum, 1)
                dve.wait_ge(x_added_sum, c + 1)
                dve.scalar_tensor_tensor(out=xc[0:p, 0:n], in0=wide(s1, p, n), scalar=-1.0 / D, in1=xv, op0=ALU.mult, op1=ALU.add).then_inc(centered, 1)
                dve.wait_ge(squared, c + 1)
                dve.tensor_reduce(var, sq[0:p, 0:n], X, ALU.add).then_inc(var_made, 1)
                dve.wait_ge(std_made, c + 1)
                dve.reciprocal(rstd, std).then_inc(rstd_made, 1)
                dve.wait_ge(rstd_made, c + 1)
                dve.wait_ge(h_turned, c + 1)
                dve.scalar_tensor_tensor(out=h[0:p, 0:n], in0=xc[0:p, 0:n], scalar=0.0, in1=wide(rstd, p, n), op0=ALU.max, op1=ALU.mult).then_inc(h_made, 1)
                dve.wait_ge(pq_copied, c + 1)
                dve.tensor_tensor(q_rest[0:p, 0:n], nodes.pq[1], q3[0:p, 0:n, 0, :], ALU.subtract).then_inc(rest_made, 1)
                dve.wait_ge(part2_made, c + 1)
                dve.tensor_tensor(q3[0:p, 0:n, 2, :], q_rest[0:p, 0:n], q3[0:p, 0:n, 1, :], ALU.subtract).then_inc(q_split, 1)

            dve.wait_ge(flag_made, 1)
            fits = dve.value_load(flag[0:1, 0:1], min_val=0, max_val=1)
            dve.wait_ge(prep_turned, 12)
            with dve.If(fits > 0):
                dve.sem_inc(window_added, AHEAD * T)
                dve.memset(acc[:, 2 * 2 * GE:3 * 2 * GE], 0.0)
                dve.memset(acc[:, 4 * 2 * GE:5 * 2 * GE], 0.0)
                chain(dve.memset(acc[:, 6 * 2 * GE:ACCN], 0.0))
                dve.wait_ge(acc_cleared, 4)
                dve.wait_ge(base_in, 32)

                def group(it, u, made=False):
                    g = it * U + u
                    if not made:
                        make_onehot0(g + 1, (u + 1) % 2)
                    _, bases = nc.values_load_multi_w_load_instructions(
                        base_row[0:1, bass.ds(g, 1), :].rearrange("a g t -> a (g t)"), engines=[ENG.DVE], min_val=0, max_val=N - 1,
                        skip_runtime_bounds_check_because="dst holds nodes' numbers")
                    dve.wait_ge(typed, AHEAD + g + 1)
                    for t in range(T):
                        window = acc[0:D, bass.ds(bases[t], W0)]
                        dve.wait_ge(window_added, AHEAD * T + g * T + t)
                        dve.tensor_tensor(window, window, node_ps[:, u % 2, t * W0:(t + 1) * W0], ALU.add).then_inc(window_added, 1)

                for u in range(U):
                    group(0, u, made=(u == 0))
                segments(dve, group, chunk_pq, begin=1)
                dve.wait_ge(window_added, (AHEAD + G) * T)
                dve.sem_inc(layer0_summed, 1)
            with dve.Else():
                dve.wait_ge(acc_cleared, 4)
                scattered_sums(dve, 0)
                dve.sem_inc(layer0_summed, 1)
                all_chunks(dve, chunk_pq)
            chunk_pq(NC, last_nodes)

            def chunk_out(c, nodes):
                xv = xs[0:nodes.p, (slice(NC * CI, NCOL) if nodes is last_nodes else bass.ds(c * CI, CI)), :]
                dve.wait_ge(out_made, c + 2)
                dve.tensor_tensor(xv, xv, nodes.out, ALU.add).then_inc(out_added, 1)

            dve.wait_ge(staged, NC + 1)
            with dve.If(fits > 0):
                dve.sem_inc(pre_added, AHEAD)
                oh1 = onehot[:, :, :, 0:P]

                def make_onehot1(g, b):
                    dve.wait_ge(z_made, AHEAD + g - 1)
                    dve.tensor_tensor(oh1[:, b], key1[:, bass.ds(g, 1), :].rearrange("p a (t c) -> p (a t) c", c=1).broadcast_to([P, T, P]),
                                      iota_f[:, 0:P].rearrange("p (a c) -> p a c", a=1).broadcast_to([P, T, P]), ALU.is_equal).then_inc(onehot1, 1)

                dve.wait_ge(prep_copied, 12)
                make_onehot1(0, 0)
                dve.memset(acc[:], 0.0).then_inc(z_added, AHEAD)

                def group(it, u):
                    g, b = it * U + u, u % 2
                    make_onehot1(g + 1, (u + 1) % 2)
                    base = dve.value_load(base_row[0:1, bass.ds(g, 1), 0], min_val=0, max_val=N - 1)
                    dve.wait_ge(pre_made, AHEAD + g + 1)
                    dve.wait_ge(rows_in[u], 16 * T * (NIT + it + 1))
                    dve.wait_ge(relu_made, g + AHEAD - 1)
                    dve.tensor_tensor(presum[:, b, 0:T * D], pre_ps[:, b, :], rows[:, u].rearrange("p t d -> p (t d)"), ALU.add).then_inc(pre_added, 1)
                    dve.wait_ge(z_made, AHEAD + g + 1)
                    window = acc[0:KA, bass.ds(base, W1N)]
                    dve.wait_ge(z_added, AHEAD + g)
                    dve.tensor_tensor(window, window, z_ps[:, b, 0:W1N], ALU.add).then_inc(z_added, 1)

                segments(dve, group, chunk_out)
                dve.wait_ge(z_added, AHEAD + G)
                dve.sem_inc(layer1_summed, 1)
            with dve.Else():
                scattered_sums(dve, 1)
                dve.sem_inc(layer1_summed, 1)
                all_chunks(dve, chunk_out)
            chunk_out(NC, last_nodes)

        @block.tensor
        def _(pe):
            for s, n in ((slots_summed, 2 * AHEAD), (typed, AHEAD), (pre_made, AHEAD), (z_made, AHEAD), (group_turned, AHEAD),
                         (turned, 1), (h_turned, 1), (pq_made, 1), (out_made, 1)):
                pe.sem_inc(s, n)
            pe.wait_ge(consts_made, 1)
            pe.wait_ge(first_float, 1)
            pe.transpose(ps[:, 5, 0:EG * T], first_f[:], ident[0:EG * T, 0:EG * T]).then_inc(first_turned, 1)
            for n in range(12):
                v = (src_f, key0_g, key1_g)[n // 4][:, n // 2 % 2, :]
                v = v.rearrange("g (p j) -> g j p", j=T) if n >= 8 else v.rearrange("g (t p) -> g t p", p=P)
                if n == 0:
                    pe.wait_ge(src_float, 1)
                if n == 4:
                    pe.wait_ge(bad_made, 1)
                    pe.matmul(ps[0:1, 4, 0:1], extremes[0:HG, 5:6], ones[0:HG, :], start=True, stop=True).then_inc(bad_summed, 1)
                if n in (4, 8):
                    pe.wait_ge(keys_made, n // 4)
                if n >= 4:
                    pe.wait_ge(prep_copied, n - 3)
                for t in range(4):
                    last = pe.transpose(ps[:, n % 4, t * HG:(t + 1) * HG], v[:, n % 2 * 4 + t, :], ident[0:HG, 0:HG])
                last.then_inc(prep_turned, 1)

            def chunk_pq(c, nodes):
                p, n = nodes.p, nodes.n
                pe.wait_ge(staged, c + 1)
                wait_apart(pe, rest_made, c + 1)
                for i in range(n):
                    last = pe.transpose(nodes.x[:, i, :], nodes.stage[0:D, i, :], ident[0:D, 0:D])
                last.then_inc(turned, 1)
                wait_apart(pe, h_made, c + 1)
                for i in range(n // 2):
                    last = pe.transpose(nodes.ht[:, i, :], h[0:p, 2 * i:2 * i + 2, :].rearrange("p i d -> p (i d)"), ident[0:p, 0:p])
                last.then_inc(h_turned, 1)
                wait_apart(pe, ht_copied, c + 1)
                for a in range(2):
                    for i in range(n // 2):
                        last = pe.matmul(nodes.pq[a][:, 2 * i:2 * i + 2, :], h_t[:, i, 0:p],
                                         w1ab[:, :, a * D:(a + 1) * D], start=True, stop=True)
                    last.then_inc((p_made, pq_made)[a], 1)

            pe.wait_ge(flag_made, 1)
            fits = pe.value_load(flag[0:1, 0:1], min_val=0, max_val=1)
            pe.wait_ge(prep_copied, 12)
            pe.wait_ge(weights_in, 16 * NWL)
            with pe.If(fits > 0):
                def group(it, u, first=False):
                    g, b = it * U + u, u % 2
                    if first and u < EG:
                        pe.wait_ge(h_made_a, NA + u // PG + 1)
                    pe.wait_ge(onehot0, g + 1)
                    pe.wait_ge(rows_in[u], 16 * T * (it + 1))
                    for t in range(T):
                        for par in range(PAR):
                            last = pe.matmul(slot_ps[par * D:(par + 1) * D, b, t, :], rows[:, u, t, :],
                                             onehot[:, b, t, par * C0:(par + 1) * C0], start=True, stop=True)
                        if t % 4 == 3:
                            last.then_inc(slots_summed, 1)
                    pe.wait_ge(slots_copied, 2 * (g + 1))
                    pe.wait_ge(window_added, T * (g + AHEAD - 1))
                    for r in range(RP):
                        last = pe.matmul(node_ps[:, b, 0:T * W0], w_pairs[:, r, :], slots[:, b, :, r * W0:(r + 1) * W0],
                                         start=(r == 0), stop=(r == RP - 1))
                    last.then_inc(typed, 1)

                for u in range(U):
                    group(0, u, first=True)
                segments(pe, group, chunk_pq, begin=1)
            with pe.Else():
                scattered_products(pe, 0)
                all_chunks(pe, chunk_pq)
            chunk_pq(NC, last_nodes)

            def chunk_out(c, nodes):
                pe.wait_ge(out_staged, c + 1)
                pe.wait_ge(out_added, c + 1)
                for i in range(nodes.n):
                    last = pe.matmul(nodes.out[:, i, :], nodes.stage[0:KA, i, :], w2b[:], start=True, stop=True)
                last.then_inc(out_made, 1)

            pe.wait_ge(rest_made, NC + 2)
            with pe.If(fits > 0):
                def turn_group(g, b, at):
                    pe.wait_ge(attr_in[at[0]], 16 * at[1])
                    wait_apart(pe, onehot1, g + 1)
                    pe.transpose(attrt_ps, attr[:, at[0], :], ident[:])
                    for j in range(T):
                        last = pe.transpose(oht_ps[:, j * P:(j + 1) * P], onehot[:, b, j, 0:P], ident[:])
                    last.then_inc(group_turned, 1)

                def group(it, u):
                    g, b = it * U + u, u % 2
                    pe.wait_ge(turn_copied, 3 * (g + 1))
                    pe.wait_ge(q_in[u % V], 16 * (it * (U // V) + u // V + 1))
                    pe.wait_ge(pre_added, g + AHEAD - 1)
                    pe.matmul(pre_ps[:, b, :], attr_t[:, b, :], w_attr[:].rearrange("k j d -> k (j d)"), start=True, stop=False)
                    for j in range(T):
                        for part in range(3):
                            last = pe.matmul(pre_ps[:, b, j * D:(j + 1) * D], onehot_t[:, b, j * P:(j + 1) * P],
                                             q_win[:, u % V, part * D:(part + 1) * D], start=False, stop=(j == T - 1 and part == 2))
                    last.then_inc(pre_made, 1)
                    turn_group(g + 1, (u + 1) % 2, ((u + 1) % V, it * (U // V) + (u + 1) // V + 1))
                    pe.wait_ge(relu_made, AHEAD + g + 1)
                    pe.wait_ge(z_added, g + AHEAD - 1)
                    for j in range(T):
                        last = pe.matmul(z_ps[:, b, 0:W1N], relus[:, b, j, :], onehot[:, b, j, 0:P], start=(j == 0), stop=(j == T - 1))
                    last.then_inc(z_made, 1)

                turn_group(0, 0, (0, 1))
                segments(pe, group, chunk_out)
                pe.wait_ge(turn_copied, 3 * (G + 1))
            with pe.Else():
                scattered_products(pe, 1)
                all_chunks(pe, chunk_out)
            chunk_out(NC, last_nodes)


_INS = ['x', 'src', 'dst', 'edge_attr_8', 'edge_type_16', 'L0_gnn_weight', 'L1_gnn_W1', 'L1_gnn_b1', 'L1_gnn_W2', 'L1_gnn_b2']


def kernel(**inputs):
    import numpy as _np
    import concourse.bacc as _bacc
    from concourse import mybir as _mybir
    from concourse.bass_utils import run_bass_kernel_spmd as _run

    nc = _bacc.Bacc("TRN2", target_bir_lowering=False, num_devices=1)
    arrays, args = {}, []
    for name in _INS:
        a = _np.ascontiguousarray(inputs[name])
        arrays[f"in_{name}_dram"] = a
        args.append(nc.dram_tensor(f"in_{name}_dram", a.shape, _mybir.dt.from_np(a.dtype), kind="ExternalInput").ap())
    shape = inputs["x"].shape
    args.append(nc.dram_tensor("out_0_dram", shape, _mybir.dt.float32, kind="ExternalOutput").ap())
    gnn_kernel(nc, *args)
    r = _run(nc, [arrays], core_ids=[0])
    return r.results[0]["out_0_dram"]
```
